# Optimizing a Trainium2 kernel written in Bass

```python
import numpy as np
import jax
import jax.numpy as jnp

def _softmax(x, axis=-1):
    return jax.nn.softmax(x, axis=axis)

def _gelu(x):
    return jax.nn.gelu(x, approximate=True)

def _silu(x):
    return jax.nn.silu(x)

def _sigmoid(x):
    return jax.nn.sigmoid(x)

def _layernorm(x, axis=-1, eps=1e-05):
    m = jnp.mean(x, axis=axis, keepdims=True)
    v = jnp.var(x, axis=axis, keepdims=True)
    return (x - m) / jnp.sqrt(v + eps)

def _scatter_add(tgt, idx, src, axis=0):
    return tgt.at[idx].add(src)

def _segment_sum(src, seg, n):
    return jax.ops.segment_sum(src, seg, n)
kernel_name = 'mk_xattn_seq_d4_seqx_r8_8fb183'

def setup_inputs(seed: int=0):
    np.random.seed(seed)
    _w = jnp.asarray

    def _rec_inputs():
        import jax
        import jax.numpy as jnp
        _rk = jax.random.key(seed)
        x = 7.22e-05 + 1 * jax.random.normal(jax.random.fold_in(_rk, 1), (16, 128, 128), jnp.float32)
        _lenS = 128 - jax.random.randint(jax.random.fold_in(_rk, 7), (16,), 0, max(1, 128 // 4) + 1, jnp.int32)
        _lenS2 = 120 - jax.random.randint(jax.random.fold_in(_rk, 8), (16,), 0, max(1, 120 // 4) + 1, jnp.int32)
        _ctx_768P = jax.random.normal(jax.random.fold_in(_rk, 11), (16, 16, 96), jnp.float32)
        _ctx_768c = jax.random.dirichlet(jax.random.fold_in(_rk, 511), 0.3 * jnp.ones((16,), jnp.float32), (16, 120))
        _ctx_768t = jnp.einsum('bsk,bkd->bsd', _ctx_768c, _ctx_768P)
        _ctx_768t = _ctx_768t * jax.lax.rsqrt(jnp.mean(jnp.square(_ctx_768t)) + 1e-12) * 0.953939
        ctx_768 = -0.00055796 + 0.999787 * (_ctx_768t + 0.3 * jax.random.normal(jax.random.fold_in(_rk, 611), (16, 120, 96), jnp.float32))
        return (x, ctx_768)
    x, ctx_768 = _rec_inputs()

    def _L0_xattn_setup():
        import jax, jax.numpy as jnp
        import numpy as np
        D_MODEL = 128
        D_COND = 96
        N_HEADS = 16
        D_HEAD = 64
        D_ATTN = N_HEADS * D_HEAD
        D_FF = 4 * D_MODEL

        def _layernorm(x, g, b, eps=1e-05):
            mu = jnp.mean(x, axis=-1, keepdims=True)
            var = jnp.var(x, axis=-1, keepdims=True)
            return (x - mu) * jax.lax.rsqrt(var + eps) * g + b

        def _attention(xq, xkv, wq, wk, wv, wo, bo):
            B, S, _ = xq.shape
            T = xkv.shape[1]
            q = (xq @ wq).reshape(B, S, N_HEADS, D_HEAD)
            k = (xkv @ wk).reshape(B, T, N_HEADS, D_HEAD)
            v = (xkv @ wv).reshape(B, T, N_HEADS, D_HEAD)
            scale = D_HEAD ** (-0.5)
            attn = jnp.einsum('bihd,bjhd->bhij', q, k) * scale
            attn = jax.nn.softmax(attn, axis=-1)
            out = jnp.einsum('bhij,bjhd->bihd', attn, v).reshape(B, S, D_ATTN)
            return out @ wo + bo
        key = jax.random.key(seed)
        ks = jax.random.split(key, 16)
        B, S, T = (8, 128, 32)
        n = jax.random.normal
        inp = {'x': n(ks[0], (B, S, D_MODEL), jnp.float32), 'cond_emb': n(ks[1], (B, T, D_COND), jnp.float32), 'ln1_g': jnp.ones((D_MODEL,), jnp.float32), 'ln1_b': jnp.zeros((D_MODEL,), jnp.float32), 'ln2_g': jnp.ones((D_MODEL,), jnp.float32), 'ln2_b': jnp.zeros((D_MODEL,), jnp.float32), 'ln3_g': jnp.ones((D_MODEL,), jnp.float32), 'ln3_b': jnp.zeros((D_MODEL,), jnp.float32), 'sa_wq': n(ks[2], (D_MODEL, D_ATTN), jnp.float32) * D_MODEL ** (-0.5), 'sa_wk': n(ks[3], (D_MODEL, D_ATTN), jnp.float32) * D_MODEL ** (-0.5), 'sa_wv': n(ks[4], (D_MODEL, D_ATTN), jnp.float32) * D_MODEL ** (-0.5), 'sa_wo': n(ks[5], (D_ATTN, D_MODEL), jnp.float32) * D_ATTN ** (-0.5), 'sa_bo': jnp.zeros((D_MODEL,), jnp.float32), 'ca_wq': n(ks[6], (D_MODEL, D_ATTN), jnp.float32) * D_MODEL ** (-0.5), 'ca_wk': n(ks[7], (D_COND, D_ATTN), jnp.float32) * D_COND ** (-0.5), 'ca_wv': n(ks[8], (D_COND, D_ATTN), jnp.float32) * D_COND ** (-0.5), 'ca_wo': n(ks[9], (D_ATTN, D_MODEL), jnp.float32) * D_ATTN ** (-0.5), 'ca_bo': jnp.zeros((D_MODEL,), jnp.float32), 'ff_w1': n(ks[10], (D_MODEL, 2 * D_FF), jnp.float32) * D_MODEL ** (-0.5), 'ff_b1': jnp.zeros((2 * D_FF,), jnp.float32), 'ff_w2': n(ks[11], (D_FF, D_MODEL), jnp.float32) * D_FF ** (-0.5), 'ff_b2': jnp.zeros((D_MODEL,), jnp.float32)}
        return inp
    _L0_xattn_all = _L0_xattn_setup()
    _L0_xattn_in = {k: v for k, v in _L0_xattn_all.items() if k in ('ln1_g', 'ln1_b', 'ln2_g', 'ln2_b', 'ln3_g', 'ln3_b', 'sa_wq', 'sa_wk', 'sa_wv', 'sa_wo', 'sa_bo', 'ca_wq', 'ca_wk', 'ca_wv', 'ca_wo', 'ca_bo', 'ff_w1', 'ff_b1', 'ff_w2', 'ff_b2')}
    del _L0_xattn_all

    def _L1_xattn_setup():
        import jax, jax.numpy as jnp
        import numpy as np
        EPS = 1e-05

        def _ln(x, g, b):
            m = jnp.mean(x, axis=-1, keepdims=True)
            v = jnp.var(x, axis=-1, keepdims=True)
            return (x - m) * jax.lax.rsqrt(v + EPS) * g + b

        def _attn(x, ctx, wq, wk, wv, wo, bo, num_heads):
            B, T, _ = x.shape
            S = ctx.shape[1]
            E = wq.shape[1]
            hd = E // num_heads
            q = (x @ wq).reshape(B, T, num_heads, hd)
            k = (ctx @ wk).reshape(B, S, num_heads, hd)
            v = (ctx @ wv).reshape(B, S, num_heads, hd)
            scores = jnp.einsum('bthd,bshd->bhts', q, k) / np.sqrt(hd).astype(x.dtype)
            p = jax.nn.softmax(scores, axis=-1)
            o = jnp.einsum('bhts,bshd->bthd', p, v).reshape(B, T, E)
            return o @ wo + bo

        def _ffn(x, w1, b1, w2, b2):
            h = jax.nn.gelu(x @ w1 + b1, approximate=False)
            return h @ w2 + b2
        key = jax.random.key(seed)
        H, CD, FF = (128, 96, 512)
        ks = jax.random.split(key, 20)
        s = 0.02
        inp = {'x': jax.random.normal(ks[0], (4, 128, H), jnp.float32), 'context': jax.random.normal(ks[1], (4, 77, CD), jnp.float32), 'sq_w': jax.random.normal(ks[2], (H, H), jnp.float32) * s, 'sk_w': jax.random.normal(ks[3], (H, H), jnp.float32) * s, 'sv_w': jax.random.normal(ks[4], (H, H), jnp.float32) * s, 'so_w': jax.random.normal(ks[5], (H, H), jnp.float32) * s, 'so_b': jnp.zeros((H,), jnp.float32), 'cq_w': jax.random.normal(ks[6], (H, H), jnp.float32) * s, 'ck_w': jax.random.normal(ks[7], (CD, H), jnp.float32) * s, 'cv_w': jax.random.normal(ks[8], (CD, H), jnp.float32) * s, 'co_w': jax.random.normal(ks[9], (H, H), jnp.float32) * s, 'co_b': jnp.zeros((H,), jnp.float32), 'n1_g': jnp.ones((H,), jnp.float32), 'n1_b': jnp.zeros((H,), jnp.float32), 'n2_g': jnp.ones((H,), jnp.float32), 'n2_b': jnp.zeros((H,), jnp.float32), 'n3_g': jnp.ones((H,), jnp.float32), 'n3_b': jnp.zeros((H,), jnp.float32), 'n4_g': jnp.ones((H,), jnp.float32), 'n4_b': jnp.zeros((H,), jnp.float32), 'f1_w1': jax.random.normal(ks[10], (H, FF), jnp.float32) * s, 'f1_b1': jnp.zeros((FF,), jnp.float32), 'f1_w2': jax.random.normal(ks[11], (FF, H), jnp.float32) * s, 'f1_b2': jnp.zeros((H,), jnp.float32), 'f2_w1': jax.random.normal(ks[12], (H, FF), jnp.float32) * s, 'f2_b1': jnp.zeros((FF,), jnp.float32), 'f2_w2': jax.random.normal(ks[13], (FF, H), jnp.float32) * s, 'f2_b2': jnp.zeros((H,), jnp.float32)}
        return inp
    _L1_xattn_all = _L1_xattn_setup()
    _L1_xattn_in = {k: v for k, v in _L1_xattn_all.items() if k in ('sq_w', 'sk_w', 'sv_w', 'so_w', 'so_b', 'cq_w', 'ck_w', 'cv_w', 'co_w', 'co_b', 'n1_g', 'n1_b', 'n2_g', 'n2_b', 'n3_g', 'n3_b', 'n4_g', 'n4_b', 'f1_w1', 'f1_b1', 'f1_w2', 'f1_b2', 'f2_w1', 'f2_b1', 'f2_w2', 'f2_b2')}
    del _L1_xattn_all

    def _L2_xattn_setup():
        import jax, jax.numpy as jnp
        import numpy as np
        DIM, HEADS, DHEAD, CTX_DIM = (128, 16, 64, 96)
        INNER = HEADS * DHEAD
        FF_HID = 4 * DIM
        EPS = 1e-05

        def _ln(x, g, b):
            mu = jnp.mean(x, axis=-1, keepdims=True)
            var = jnp.mean(jnp.square(x - mu), axis=-1, keepdims=True)
            return (x - mu) * jax.lax.rsqrt(var + EPS) * g + b

        def _attn(x, ctx, Wq, Wk, Wv, Wo, bo):
            b, n, _ = x.shape
            m = ctx.shape[1]
            q = (x @ Wq).reshape(b, n, HEADS, DHEAD)
            k = (ctx @ Wk).reshape(b, m, HEADS, DHEAD)
            v = (ctx @ Wv).reshape(b, m, HEADS, DHEAD)
            scale = DHEAD ** (-0.5)
            sim = jnp.einsum('bihd,bjhd->bhij', q, k) * scale
            attn = jax.nn.softmax(sim, axis=-1)
            out = jnp.einsum('bhij,bjhd->bihd', attn, v).reshape(b, n, INNER)
            return out @ Wo + bo
        key = jax.random.key(seed)
        ks = jax.random.split(key, 24)

        def w(k, shape, fan_in):
            return jax.random.normal(k, shape, jnp.float32) * fan_in ** (-0.5)
        inp = {'x': jax.random.normal(ks[0], (2, 256, DIM), jnp.float32), 'context': jax.random.normal(ks[1], (2, 77, CTX_DIM), jnp.float32), 'Wq1': w(ks[2], (DIM, INNER), DIM), 'Wk1': w(ks[3], (DIM, INNER), DIM), 'Wv1': w(ks[4], (DIM, INNER), DIM), 'Wo1': w(ks[5], (INNER, DIM), INNER), 'bo1': jnp.zeros((DIM,), jnp.float32), 'Wq2': w(ks[6], (DIM, INNER), DIM), 'Wk2': w(ks[7], (CTX_DIM, INNER), CTX_DIM), 'Wv2': w(ks[8], (CTX_DIM, INNER), CTX_DIM), 'Wo2': w(ks[9], (INNER, DIM), INNER), 'bo2': jnp.zeros((DIM,), jnp.float32), 'Wp': w(ks[10], (DIM, 2 * FF_HID), DIM), 'bp': jnp.zeros((2 * FF_HID,), jnp.float32), 'W2': w(ks[11], (FF_HID, DIM), FF_HID), 'b2': jnp.zeros((DIM,), jnp.float32), 'g1': jnp.ones((DIM,), jnp.float32), 'be1': jnp.zeros((DIM,), jnp.float32), 'g2': jnp.ones((DIM,), jnp.float32), 'be2': jnp.zeros((DIM,), jnp.float32), 'g3': jnp.ones((DIM,), jnp.float32), 'be3': jnp.zeros((DIM,), jnp.float32)}
        return inp
    _L2_xattn_all = _L2_xattn_setup()
    _L2_xattn_in = {k: v for k, v in _L2_xattn_all.items() if k in ('Wq1', 'Wk1', 'Wv1', 'Wo1', 'bo1', 'Wq2', 'Wk2', 'Wv2', 'Wo2', 'bo2', 'Wp', 'bp', 'W2', 'b2', 'g1', 'be1', 'g2', 'be2', 'g3', 'be3')}
    del _L2_xattn_all

    def _L3_xattn_setup():
        import jax, jax.numpy as jnp
        import numpy as np
        DEPTH = 4
        DIM = 128
        HEADS = 16
        DIM_HEAD = 64
        INNER = HEADS * DIM_HEAD
        MLP = 512
        CTX = 96
        SCALE = DIM_HEAD ** (-0.5)
        EPS = 1e-05

        def _ln(x, g, b):
            mu = jnp.mean(x, axis=-1, keepdims=True)
            var = jnp.mean(jnp.square(x - mu), axis=-1, keepdims=True)
            return (x - mu) * jax.lax.rsqrt(var + EPS) * g + b

        def _heads(t):
            b, n, _ = t.shape
            return t.reshape(b, n, HEADS, DIM_HEAD).transpose(0, 2, 1, 3)

        def _mha(q, k, v):
            attn = jax.nn.softmax(jnp.einsum('bhqd,bhkd->bhqk', q, k) * SCALE, axis=-1)
            out = jnp.einsum('bhqk,bhkd->bhqd', attn, v)
            b, h, n, d = out.shape
            return out.transpose(0, 2, 1, 3).reshape(b, n, h * d)
        key = jax.random.key(seed)
        ks = jax.random.split(key, 12)

        def rn(k, shape, s=0.02):
            return jax.random.normal(k, shape, jnp.float32) * s
        return {'x': jax.random.normal(ks[0], (2, 256, DIM), jnp.float32), 'context': jax.random.normal(ks[1], (2, 128, CTX), jnp.float32), 'ln1_g': jnp.ones((DEPTH, DIM), jnp.float32), 'ln1_b': jnp.zeros((DEPTH, DIM), jnp.float32), 'w_qkv': rn(ks[2], (DEPTH, DIM, 3 * INNER)), 'w_sa_o': rn(ks[3], (DEPTH, INNER, DIM)), 'b_sa_o': jnp.zeros((DEPTH, DIM), jnp.float32), 'ln2_g': jnp.ones((DEPTH, DIM), jnp.float32), 'ln2_b': jnp.zeros((DEPTH, DIM), jnp.float32), 'w_q': rn(ks[4], (DEPTH, DIM, INNER)), 'w_kv': rn(ks[5], (DEPTH, CTX, 2 * INNER)), 'w_ca_o': rn(ks[6], (DEPTH, INNER, DIM)), 'b_ca_o': jnp.zeros((DEPTH, DIM), jnp.float32), 'ln3_g': jnp.ones((DEPTH, DIM), jnp.float32), 'ln3_b': jnp.zeros((DEPTH, DIM), jnp.float32), 'w_ff1': rn(ks[7], (DEPTH, DIM, MLP)), 'b_ff1': jnp.zeros((DEPTH, MLP), jnp.float32), 'w_ff2': rn(ks[8], (DEPTH, MLP, DIM)), 'b_ff2': jnp.zeros((DEPTH, DIM), jnp.float32)}
    _L3_xattn_all = _L3_xattn_setup()
    _L3_xattn_in = {k: v for k, v in _L3_xattn_all.items() if k in ('ln1_g', 'ln1_b', 'w_qkv', 'w_sa_o', 'b_sa_o', 'ln2_g', 'ln2_b', 'w_q', 'w_kv', 'w_ca_o', 'b_ca_o', 'ln3_g', 'ln3_b', 'w_ff1', 'b_ff1', 'w_ff2', 'b_ff2')}
    del _L3_xattn_all
    return {'x': x, 'ctx_768': ctx_768, 'L0_xattn_ln1_g': _L0_xattn_in['ln1_g'], 'L0_xattn_ln1_b': _L0_xattn_in['ln1_b'], 'L0_xattn_ln2_g': _L0_xattn_in['ln2_g'], 'L0_xattn_ln2_b': _L0_xattn_in['ln2_b'], 'L0_xattn_ln3_g': _L0_xattn_in['ln3_g'], 'L0_xattn_ln3_b': _L0_xattn_in['ln3_b'], 'L0_xattn_sa_wq': _L0_xattn_in['sa_wq'], 'L0_xattn_sa_wk': _L0_xattn_in['sa_wk'], 'L0_xattn_sa_wv': _L0_xattn_in['sa_wv'], 'L0_xattn_sa_wo': _L0_xattn_in['sa_wo'], 'L0_xattn_sa_bo': _L0_xattn_in['sa_bo'], 'L0_xattn_ca_wq': _L0_xattn_in['ca_wq'], 'L0_xattn_ca_wk': _L0_xattn_in['ca_wk'], 'L0_xattn_ca_wv': _L0_xattn_in['ca_wv'], 'L0_xattn_ca_wo': _L0_xattn_in['ca_wo'], 'L0_xattn_ca_bo': _L0_xattn_in['ca_bo'], 'L0_xattn_ff_w1': _L0_xattn_in['ff_w1'], 'L0_xattn_ff_b1': _L0_xattn_in['ff_b1'], 'L0_xattn_ff_w2': _L0_xattn_in['ff_w2'], 'L0_xattn_ff_b2': _L0_xattn_in['ff_b2'], 'L1_xattn_sq_w': _L1_xattn_in['sq_w'], 'L1_xattn_sk_w': _L1_xattn_in['sk_w'], 'L1_xattn_sv_w': _L1_xattn_in['sv_w'], 'L1_xattn_so_w': _L1_xattn_in['so_w'], 'L1_xattn_so_b': _L1_xattn_in['so_b'], 'L1_xattn_cq_w': _L1_xattn_in['cq_w'], 'L1_xattn_ck_w': _L1_xattn_in['ck_w'], 'L1_xattn_cv_w': _L1_xattn_in['cv_w'], 'L1_xattn_co_w': _L1_xattn_in['co_w'], 'L1_xattn_co_b': _L1_xattn_in['co_b'], 'L1_xattn_n1_g': _L1_xattn_in['n1_g'], 'L1_xattn_n1_b': _L1_xattn_in['n1_b'], 'L1_xattn_n2_g': _L1_xattn_in['n2_g'], 'L1_xattn_n2_b': _L1_xattn_in['n2_b'], 'L1_xattn_n3_g': _L1_xattn_in['n3_g'], 'L1_xattn_n3_b': _L1_xattn_in['n3_b'], 'L1_xattn_n4_g': _L1_xattn_in['n4_g'], 'L1_xattn_n4_b': _L1_xattn_in['n4_b'], 'L1_xattn_f1_w1': _L1_xattn_in['f1_w1'], 'L1_xattn_f1_b1': _L1_xattn_in['f1_b1'], 'L1_xattn_f1_w2': _L1_xattn_in['f1_w2'], 'L1_xattn_f1_b2': _L1_xattn_in['f1_b2'], 'L1_xattn_f2_w1': _L1_xattn_in['f2_w1'], 'L1_xattn_f2_b1': _L1_xattn_in['f2_b1'], 'L1_xattn_f2_w2': _L1_xattn_in['f2_w2'], 'L1_xattn_f2_b2': _L1_xattn_in['f2_b2'], 'L2_xattn_Wq1': _L2_xattn_in['Wq1'], 'L2_xattn_Wk1': _L2_xattn_in['Wk1'], 'L2_xattn_Wv1': _L2_xattn_in['Wv1'], 'L2_xattn_Wo1': _L2_xattn_in['Wo1'], 'L2_xattn_bo1': _L2_xattn_in['bo1'], 'L2_xattn_Wq2': _L2_xattn_in['Wq2'], 'L2_xattn_Wk2': _L2_xattn_in['Wk2'], 'L2_xattn_Wv2': _L2_xattn_in['Wv2'], 'L2_xattn_Wo2': _L2_xattn_in['Wo2'], 'L2_xattn_bo2': _L2_xattn_in['bo2'], 'L2_xattn_Wp': _L2_xattn_in['Wp'], 'L2_xattn_bp': _L2_xattn_in['bp'], 'L2_xattn_W2': _L2_xattn_in['W2'], 'L2_xattn_b2': _L2_xattn_in['b2'], 'L2_xattn_g1': _L2_xattn_in['g1'], 'L2_xattn_be1': _L2_xattn_in['be1'], 'L2_xattn_g2': _L2_xattn_in['g2'], 'L2_xattn_be2': _L2_xattn_in['be2'], 'L2_xattn_g3': _L2_xattn_in['g3'], 'L2_xattn_be3': _L2_xattn_in['be3'], 'L3_xattn_ln1_g': _L3_xattn_in['ln1_g'], 'L3_xattn_ln1_b': _L3_xattn_in['ln1_b'], 'L3_xattn_w_qkv': _L3_xattn_in['w_qkv'], 'L3_xattn_w_sa_o': _L3_xattn_in['w_sa_o'], 'L3_xattn_b_sa_o': _L3_xattn_in['b_sa_o'], 'L3_xattn_ln2_g': _L3_xattn_in['ln2_g'], 'L3_xattn_ln2_b': _L3_xattn_in['ln2_b'], 'L3_xattn_w_q': _L3_xattn_in['w_q'], 'L3_xattn_w_kv': _L3_xattn_in['w_kv'], 'L3_xattn_w_ca_o': _L3_xattn_in['w_ca_o'], 'L3_xattn_b_ca_o': _L3_xattn_in['b_ca_o'], 'L3_xattn_ln3_g': _L3_xattn_in['ln3_g'], 'L3_xattn_ln3_b': _L3_xattn_in['ln3_b'], 'L3_xattn_w_ff1': _L3_xattn_in['w_ff1'], 'L3_xattn_b_ff1': _L3_xattn_in['b_ff1'], 'L3_xattn_w_ff2': _L3_xattn_in['w_ff2'], 'L3_xattn_b_ff2': _L3_xattn_in['b_ff2']}

def reference(x, ctx_768, L0_xattn_ln1_g, L0_xattn_ln1_b, L0_xattn_ln2_g, L0_xattn_ln2_b, L0_xattn_ln3_g, L0_xattn_ln3_b, L0_xattn_sa_wq, L0_xattn_sa_wk, L0_xattn_sa_wv, L0_xattn_sa_wo, L0_xattn_sa_bo, L0_xattn_ca_wq, L0_xattn_ca_wk, L0_xattn_ca_wv, L0_xattn_ca_wo, L0_xattn_ca_bo, L0_xattn_ff_w1, L0_xattn_ff_b1, L0_xattn_ff_w2, L0_xattn_ff_b2, L1_xattn_sq_w, L1_xattn_sk_w, L1_xattn_sv_w, L1_xattn_so_w, L1_xattn_so_b, L1_xattn_cq_w, L1_xattn_ck_w, L1_xattn_cv_w, L1_xattn_co_w, L1_xattn_co_b, L1_xattn_n1_g, L1_xattn_n1_b, L1_xattn_n2_g, L1_xattn_n2_b, L1_xattn_n3_g, L1_xattn_n3_b, L1_xattn_n4_g, L1_xattn_n4_b, L1_xattn_f1_w1, L1_xattn_f1_b1, L1_xattn_f1_w2, L1_xattn_f1_b2, L1_xattn_f2_w1, L1_xattn_f2_b1, L1_xattn_f2_w2, L1_xattn_f2_b2, L2_xattn_Wq1, L2_xattn_Wk1, L2_xattn_Wv1, L2_xattn_Wo1, L2_xattn_bo1, L2_xattn_Wq2, L2_xattn_Wk2, L2_xattn_Wv2, L2_xattn_Wo2, L2_xattn_bo2, L2_xattn_Wp, L2_xattn_bp, L2_xattn_W2, L2_xattn_b2, L2_xattn_g1, L2_xattn_be1, L2_xattn_g2, L2_xattn_be2, L2_xattn_g3, L2_xattn_be3, L3_xattn_ln1_g, L3_xattn_ln1_b, L3_xattn_w_qkv, L3_xattn_w_sa_o, L3_xattn_b_sa_o, L3_xattn_ln2_g, L3_xattn_ln2_b, L3_xattn_w_q, L3_xattn_w_kv, L3_xattn_w_ca_o, L3_xattn_b_ca_o, L3_xattn_ln3_g, L3_xattn_ln3_b, L3_xattn_w_ff1, L3_xattn_b_ff1, L3_xattn_w_ff2, L3_xattn_b_ff2):
    import jax
    import jax.numpy as jnp

    def _L0_xattn_ref(x, cond_emb, ln1_g, ln1_b, ln2_g, ln2_b, ln3_g, ln3_b, sa_wq, sa_wk, sa_wv, sa_wo, sa_bo, ca_wq, ca_wk, ca_wv, ca_wo, ca_bo, ff_w1, ff_b1, ff_w2, ff_b2):
        import jax, jax.numpy as jnp
        import numpy as np
        D_MODEL = 128
        D_COND = 96
        N_HEADS = 16
        D_HEAD = 64
        D_ATTN = N_HEADS * D_HEAD
        D_FF = 4 * D_MODEL

        def _layernorm(x, g, b, eps=1e-05):
            mu = jnp.mean(x, axis=-1, keepdims=True)
            var = jnp.var(x, axis=-1, keepdims=True)
            return (x - mu) * jax.lax.rsqrt(var + eps) * g + b

        def _attention(xq, xkv, wq, wk, wv, wo, bo):
            B, S, _ = xq.shape
            T = xkv.shape[1]
            q = (xq @ wq).reshape(B, S, N_HEADS, D_HEAD)
            k = (xkv @ wk).reshape(B, T, N_HEADS, D_HEAD)
            v = (xkv @ wv).reshape(B, T, N_HEADS, D_HEAD)
            scale = D_HEAD ** (-0.5)
            attn = jnp.einsum('bihd,bjhd->bhij', q, k) * scale
            attn = jax.nn.softmax(attn, axis=-1)
            out = jnp.einsum('bhij,bjhd->bihd', attn, v).reshape(B, S, D_ATTN)
            return out @ wo + bo
        h = _layernorm(x, ln1_g, ln1_b)
        x = _attention(h, h, sa_wq, sa_wk, sa_wv, sa_wo, sa_bo) + x
        h = _layernorm(x, ln2_g, ln2_b)
        x = _attention(h, cond_emb, ca_wq, ca_wk, ca_wv, ca_wo, ca_bo) + x
        h = _layernorm(x, ln3_g, ln3_b)
        p = h @ ff_w1 + ff_b1
        a, gate = (p[..., :D_FF], p[..., D_FF:])
        h = a * jax.nn.gelu(gate, approximate=False) @ ff_w2 + ff_b2
        return h + x

    def _L1_xattn_ref(x, context, sq_w, sk_w, sv_w, so_w, so_b, cq_w, ck_w, cv_w, co_w, co_b, n1_g, n1_b, n2_g, n2_b, n3_g, n3_b, n4_g, n4_b, f1_w1, f1_b1, f1_w2, f1_b2, f2_w1, f2_b1, f2_w2, f2_b2):
        import jax, jax.numpy as jnp
        import numpy as np
        EPS = 1e-05

        def _ln(x, g, b):
            m = jnp.mean(x, axis=-1, keepdims=True)
            v = jnp.var(x, axis=-1, keepdims=True)
            return (x - m) * jax.lax.rsqrt(v + EPS) * g + b

        def _attn(x, ctx, wq, wk, wv, wo, bo, num_heads):
            B, T, _ = x.shape
            S = ctx.shape[1]
            E = wq.shape[1]
            hd = E // num_heads
            q = (x @ wq).reshape(B, T, num_heads, hd)
            k = (ctx @ wk).reshape(B, S, num_heads, hd)
            v = (ctx @ wv).reshape(B, S, num_heads, hd)
            scores = jnp.einsum('bthd,bshd->bhts', q, k) / np.sqrt(hd).astype(x.dtype)
            p = jax.nn.softmax(scores, axis=-1)
            o = jnp.einsum('bhts,bshd->bthd', p, v).reshape(B, T, E)
            return o @ wo + bo

        def _ffn(x, w1, b1, w2, b2):
            h = jax.nn.gelu(x @ w1 + b1, approximate=False)
            return h @ w2 + b2
        NUM_HEADS = 16
        x = _attn(_ln(x, n1_g, n1_b), _ln(x, n1_g, n1_b), sq_w, sk_w, sv_w, so_w, so_b, NUM_HEADS) + x
        x = _ffn(_ln(x, n2_g, n2_b), f1_w1, f1_b1, f1_w2, f1_b2) + x
        x = _attn(_ln(x, n3_g, n3_b), context, cq_w, ck_w, cv_w, co_w, co_b, NUM_HEADS) + x
        x = _ffn(_ln(x, n4_g, n4_b), f2_w1, f2_b1, f2_w2, f2_b2) + x
        return x

    def _L2_xattn_ref(x, context, Wq1, Wk1, Wv1, Wo1, bo1, Wq2, Wk2, Wv2, Wo2, bo2, Wp, bp, W2, b2, g1, be1, g2, be2, g3, be3):
        import jax, jax.numpy as jnp
        import numpy as np
        DIM, HEADS, DHEAD, CTX_DIM = (128, 16, 64, 96)
        INNER = HEADS * DHEAD
        FF_HID = 4 * DIM
        EPS = 1e-05

        def _ln(x, g, b):
            mu = jnp.mean(x, axis=-1, keepdims=True)
            var = jnp.mean(jnp.square(x - mu), axis=-1, keepdims=True)
            return (x - mu) * jax.lax.rsqrt(var + EPS) * g + b

        def _attn(x, ctx, Wq, Wk, Wv, Wo, bo):
            b, n, _ = x.shape
            m = ctx.shape[1]
            q = (x @ Wq).reshape(b, n, HEADS, DHEAD)
            k = (ctx @ Wk).reshape(b, m, HEADS, DHEAD)
            v = (ctx @ Wv).reshape(b, m, HEADS, DHEAD)
            scale = DHEAD ** (-0.5)
            sim = jnp.einsum('bihd,bjhd->bhij', q, k) * scale
            attn = jax.nn.softmax(sim, axis=-1)
            out = jnp.einsum('bhij,bjhd->bihd', attn, v).reshape(b, n, INNER)
            return out @ Wo + bo
        h = _ln(x, g1, be1)
        x = _attn(h, h, Wq1, Wk1, Wv1, Wo1, bo1) + x
        h = _ln(x, g2, be2)
        x = _attn(h, context, Wq2, Wk2, Wv2, Wo2, bo2) + x
        h = _ln(x, g3, be3)
        y = h @ Wp + bp
        a, gate = (y[..., :FF_HID], y[..., FF_HID:])
        x = a * jax.nn.gelu(gate, approximate=False) @ W2 + b2 + x
        return x

    def _L3_xattn_ref(x, context, ln1_g, ln1_b, w_qkv, w_sa_o, b_sa_o, ln2_g, ln2_b, w_q, w_kv, w_ca_o, b_ca_o, ln3_g, ln3_b, w_ff1, b_ff1, w_ff2, b_ff2):
        import jax, jax.numpy as jnp
        import numpy as np
        DEPTH = 4
        DIM = 128
        HEADS = 16
        DIM_HEAD = 64
        INNER = HEADS * DIM_HEAD
        MLP = 512
        CTX = 96
        SCALE = DIM_HEAD ** (-0.5)
        EPS = 1e-05

        def _ln(x, g, b):
            mu = jnp.mean(x, axis=-1, keepdims=True)
            var = jnp.mean(jnp.square(x - mu), axis=-1, keepdims=True)
            return (x - mu) * jax.lax.rsqrt(var + EPS) * g + b

        def _heads(t):
            b, n, _ = t.shape
            return t.reshape(b, n, HEADS, DIM_HEAD).transpose(0, 2, 1, 3)

        def _mha(q, k, v):
            attn = jax.nn.softmax(jnp.einsum('bhqd,bhkd->bhqk', q, k) * SCALE, axis=-1)
            out = jnp.einsum('bhqk,bhkd->bhqd', attn, v)
            b, h, n, d = out.shape
            return out.transpose(0, 2, 1, 3).reshape(b, n, h * d)
        for i in range(DEPTH):
            h = _ln(x, ln1_g[i], ln1_b[i])
            qkv = h @ w_qkv[i]
            q, k, v = jnp.split(qkv, 3, axis=-1)
            sa = _mha(_heads(q), _heads(k), _heads(v)) @ w_sa_o[i] + b_sa_o[i]
            x = sa + x
            h = _ln(x, ln2_g[i], ln2_b[i])
            q = h @ w_q[i]
            kv = context @ w_kv[i]
            k, v = jnp.split(kv, 2, axis=-1)
            ca = _mha(_heads(q), _heads(k), _heads(v)) @ w_ca_o[i] + b_ca_o[i]
            x = ca + x
            h = _ln(x, ln3_g[i], ln3_b[i])
            ff = jax.nn.gelu(h @ w_ff1[i] + b_ff1[i], approximate=False) @ w_ff2[i] + b_ff2[i]
            x = ff + x
        return x
    x = _L0_xattn_ref(x, ctx_768, L0_xattn_ln1_g, L0_xattn_ln1_b, L0_xattn_ln2_g, L0_xattn_ln2_b, L0_xattn_ln3_g, L0_xattn_ln3_b, L0_xattn_sa_wq, L0_xattn_sa_wk, L0_xattn_sa_wv, L0_xattn_sa_wo, L0_xattn_sa_bo, L0_xattn_ca_wq, L0_xattn_ca_wk, L0_xattn_ca_wv, L0_xattn_ca_wo, L0_xattn_ca_bo, L0_xattn_ff_w1, L0_xattn_ff_b1, L0_xattn_ff_w2, L0_xattn_ff_b2)
    x = _L1_xattn_ref(x, ctx_768, L1_xattn_sq_w, L1_xattn_sk_w, L1_xattn_sv_w, L1_xattn_so_w, L1_xattn_so_b, L1_xattn_cq_w, L1_xattn_ck_w, L1_xattn_cv_w, L1_xattn_co_w, L1_xattn_co_b, L1_xattn_n1_g, L1_xattn_n1_b, L1_xattn_n2_g, L1_xattn_n2_b, L1_xattn_n3_g, L1_xattn_n3_b, L1_xattn_n4_g, L1_xattn_n4_b, L1_xattn_f1_w1, L1_xattn_f1_b1, L1_xattn_f1_w2, L1_xattn_f1_b2, L1_xattn_f2_w1, L1_xattn_f2_b1, L1_xattn_f2_w2, L1_xattn_f2_b2)
    x = _L2_xattn_ref(x, ctx_768, L2_xattn_Wq1, L2_xattn_Wk1, L2_xattn_Wv1, L2_xattn_Wo1, L2_xattn_bo1, L2_xattn_Wq2, L2_xattn_Wk2, L2_xattn_Wv2, L2_xattn_Wo2, L2_xattn_bo2, L2_xattn_Wp, L2_xattn_bp, L2_xattn_W2, L2_xattn_b2, L2_xattn_g1, L2_xattn_be1, L2_xattn_g2, L2_xattn_be2, L2_xattn_g3, L2_xattn_be3)
    x = _L3_xattn_ref(x, ctx_768, L3_xattn_ln1_g, L3_xattn_ln1_b, L3_xattn_w_qkv, L3_xattn_w_sa_o, L3_xattn_b_sa_o, L3_xattn_ln2_g, L3_xattn_ln2_b, L3_xattn_w_q, L3_xattn_w_kv, L3_xattn_w_ca_o, L3_xattn_b_ca_o, L3_xattn_ln3_g, L3_xattn_ln3_b, L3_xattn_w_ff1, L3_xattn_b_ff1, L3_xattn_w_ff2, L3_xattn_b_ff2)
    return x

_drawn_inputs = setup_inputs


def setup_inputs(seed=0):
    import zlib

    import numpy as np

    out = dict(_drawn_inputs(seed))
    spreads = {'L0_xattn_ln1_g': (1.0, 0.2),
     'L0_xattn_ln1_b': (0.0, 0.1),
     'L0_xattn_ln2_g': (1.0, 0.2),
     'L0_xattn_ln2_b': (0.0, 0.325),
     'L0_xattn_ln3_g': (1.0, 0.2),
     'L0_xattn_ln3_b': (0.0, 0.1),
     'L0_xattn_sa_bo': (0.0, 0.1),
     'L0_xattn_ca_bo': (0.0, 0.1),
     'L0_xattn_ff_b1': (0.0, 0.1),
     'L0_xattn_ff_b2': (0.0, 0.1),
     'L1_xattn_so_b': (0.0, 0.1),
     'L1_xattn_co_b': (0.0, 0.1),
     'L1_xattn_n1_g': (1.0, 0.6),
     'L1_xattn_n1_b': (0.0, 0.8),
     'L1_xattn_n2_g': (1.0, 0.6),
     'L1_xattn_n2_b': (0.0, 0.8),
     'L1_xattn_n3_g': (1.0, 0.6),
     'L1_xattn_n3_b': (0.0, 0.8),
     'L1_xattn_n4_g': (1.0, 0.6),
     'L1_xattn_n4_b': (0.0, 2.0),
     'L1_xattn_f1_b1': (0.0, 0.522),
     'L1_xattn_f1_b2': (0.0, 0.1),
     'L1_xattn_f2_b1': (0.0, 0.535),
     'L1_xattn_f2_b2': (0.0, 0.1),
     'L2_xattn_bo1': (0.0, 0.1),
     'L2_xattn_bo2': (0.0, 0.1),
     'L2_xattn_bp': (0.0, 0.1),
     'L2_xattn_b2': (0.0, 0.1),
     'L2_xattn_g1': (1.0, 0.2),
     'L2_xattn_be1': (0.0, 0.1),
     'L2_xattn_g2': (1.0, 0.594),
     'L2_xattn_be2': (0.0, 0.664),
     'L2_xattn_g3': (1.0, 0.2),
     'L2_xattn_be3': (0.0, 0.1),
     'L3_xattn_ln1_g': (1.0, 0.6),
     'L3_xattn_ln1_b': (0.0, 0.63),
     'L3_xattn_b_sa_o': (0.0, 0.1),
     'L3_xattn_ln2_g': (1.0, 0.6),
     'L3_xattn_ln2_b': (0.0, 2.0),
     'L3_xattn_b_ca_o': (0.0, 0.1),
     'L3_xattn_ln3_g': (1.0, 0.6),
     'L3_xattn_ln3_b': (0.0, 0.8),
     'L3_xattn_b_ff1': (0.0, 0.395),
     'L3_xattn_b_ff2': (0.0, 0.1)}
    factors = {'L1_xattn_sq_w': 8.0,
     'L1_xattn_sk_w': 8.0,
     'L1_xattn_sv_w': 3.599,
     'L1_xattn_so_w': 3.54,
     'L1_xattn_cq_w': 8.0,
     'L1_xattn_ck_w': 8.0,
     'L1_xattn_cv_w': 3.763,
     'L1_xattn_co_w': 3.885,
     'L3_xattn_w_q': 37.275}
    for name, (base, spread) in spreads.items():
        noise = np.random.default_rng([zlib.crc32(name.encode()), seed]).standard_normal(out[name].shape)
        drawn = base * np.exp(spread * noise) if base else spread * noise
        out[name] = jnp.asarray(drawn.astype(out[name].dtype))
    for name, factor in factors.items():
        out[name] = (out[name] * factor).astype(out[name].dtype)
    return out
```

```python
from contextlib import ExitStack

import concourse.bass as bass
from concourse import mybir

F32 = mybir.dt.float32
F32R = mybir.dt.float32r
ALU = mybir.AluOpType
ACT = mybir.ActivationFunctionType
AX = mybir.AxisListType

B, S, D = 16, 128, 128
T, C = 120, 96
HEADS, SLOT = 16, 64
INNER = HEADS * SLOT
THIN = 8
FF = 4 * D
EPS = 1e-5

GB = 2
NG = B // GB
GN = GB * S
QUADS = GB * 4
CH = INNER // 128
FC = FF // 128
DEPTH3 = 4
STAGES, ATTNS, FFS = 10 + 3 * DEPTH3, 6 + 2 * DEPTH3, 4 + DEPTH3

QK_AT = {1: (0, 1), 2: (2,), 3: (3,), 4: (4,), 5: (5,), 6: (6,), 7: (7,)}
V_AT = {2: 0, 3: 1, 4: 2, 5: 3}
OUT_AT = (5, 8)
W_DMAS, FF_DMAS = 5, 2


def run_network(eng, attention, feed_forward):
    attention(0, 0, False, False)
    attention(1, 1, True, False)
    feed_forward(2, 0, True, 1)
    attention(3, 2, False, True)
    feed_forward(4, 1, False, 2)
    attention(5, 3, True, True)
    feed_forward(6, 2, False, 3)
    attention(7, 4, False, False)
    attention(8, 5, True, False)
    feed_forward(9, 3, True, 5)
    with eng.Fori(0, DEPTH3) as layer:
        attention(layer * 3 + 10, layer * 2 + 6, False, False, layer)
        attention(layer * 3 + 11, layer * 2 + 7, True, False, layer)
        feed_forward(layer * 3 + 12, layer + 4, False, layer * 2 + 7, layer)


def at_least(eng, sem, value):
    if isinstance(value, int) and value <= 0:
        return
    eng.wait_ge(sem, value)


def hold(eng, sem, value, held):
    eng.wait_ge(sem, value)
    eng.sem_inc(held, 1)


def build(nc, x, ctxT, norms, out_biases, hidden_biases, attn_w, thin_w, ff_w, deep_w, out):
    with ExitStack() as ctx:
        def sb(name, shape, dt=F32):
            return ctx.enter_context(nc.sbuf_tensor(name, shape, dt))

        def psum(name, shape):
            return ctx.enter_context(nc.psum_tensor(name, shape, F32))

        def sem(name):
            return ctx.enter_context(nc.semaphore(name))

        xs = sb("xs", [128, B, D])
        ctx_sb = sb("ctx_sb", [C, B * T])
        norm_sb = sb("norm_sb", [128, STAGES, 2])
        obias = sb("obias", [128, STAGES, D])
        hbias = sb("hbias", [128, FFS, 2 * FC])
        ident = sb("ident", [128, 128])
        half = sb("half", [128, B])
        bnst = sb("bnst", [128, 6])
        mv_row = sb("mv_row", [128, 2])
        x_row = sb("x_row", [128, D])
        mv = sb("mv", [128, B, 2])
        ve = sb("ve", [128, B])
        rstd = sb("rstd", [128, B])
        xhat = sb("xhat", [128, GB, D])
        hT = sb("hT", [128, GN])
        h_hi = sb("h_hi", [128, GN], F32R)
        h_lo = sb("h_lo", [128, GN], F32R)
        c_hi = sb("c_hi", [C, GB * T], F32R)
        c_lo = sb("c_lo", [C, GB * T], F32R)
        w_raw = sb("w_raw", [128, 3, INNER])
        w_hi = sb("w_hi", [128, 3, INNER], F32R)
        w_lo = sb("w_lo", [128, 3, INNER], F32R)
        wo_sb = sb("wo_sb", [128, 2, CH, D])
        w1_raw = sb("w1_raw", [128, 2 * FF])
        w1_hi = sb("w1_hi", [128, 2 * FF], F32R)
        w1_lo = sb("w1_lo", [128, 2 * FF], F32R)
        w2_sb = sb("w2_sb", [128, FC, D])
        qT = sb("qT", [128, 2, CH, GN])
        kT = sb("kT", [128, 2, CH, GN])
        v_sb = sb("v_sb", [128, 2, GB, INNER])
        negmax = sb("negmax", [128, 2, 4])
        sums = sb("sums", [128, 2, 4])
        rinv = sb("rinv", [128, 2, 4])
        probs = sb("probs", [128, 2, 4, S])
        pT = sb("pT", [128, 4, 4, S])
        outT = sb("outT", [128, 2, CH, S])
        hb = sb("hb", [128, 2 * FC])
        gate = sb("gate", [128, 2, GN])
        hid = sb("hid", [128, 2, FC, GN])

        score_ps = [psum(f"score_ps{i}", [128, 4, 128]) for i in range(2)]
        pT_ps = [psum(f"pT_ps{i}", [128, 4, 128]) for i in range(2)]
        o_ps = psum("o_ps", [128, 512])
        y_ps = psum("y_ps", [128, 512])
        qv_ps = psum("qv_ps", [128, 512])
        k_ps = psum("k_ps", [128, 512])

        x_loaded = sem("x_loaded")
        params_loaded = sem("params_loaded")
        w_loaded = sem("w_loaded")
        ff_loaded = sem("ff_loaded")
        pad_zeroed = sem("pad_zeroed")
        ident_zeroed = sem("ident_zeroed")
        ident_ready = sem("ident_ready")
        half_ready = sem("half_ready")
        w_hi_ready = sem("w_hi_ready")
        w_split = sem("w_split")
        w1_hi_ready = sem("w1_hi_ready")
        w1_split = sem("w1_split")
        bn_ready = sem("bn_ready")
        aggr_ready = sem("aggr_ready")
        y_taken = sem("y_taken")
        hb_ready = sem("hb_ready")
        stats_ready = sem("stats_ready")
        ve_ready = sem("ve_ready")
        rstd_ready = sem("rstd_ready")
        xhat_ready = sem("xhat_ready")
        xbias_ready = sem("xbias_ready")
        hT_in_psum = sem("hT_in_psum")
        hT_affine = sem("hT_affine")
        h_hi_ready = sem("h_hi_ready")
        hT_ready = sem("hT_ready")
        q_in_psum = sem("q_in_psum")
        k_in_psum = sem("k_in_psum")
        v_in_psum = sem("v_in_psum")
        q_ready = sem("q_ready")
        k_ready = sem("k_ready")
        v_ready = sem("v_ready")
        scores_ready = sem("scores_ready")
        negmax_ready = sem("negmax_ready")
        exp_ready = sem("exp_ready")
        rinv_ready = sem("rinv_ready")
        probs_ready = sem("probs_ready")
        pT_in_psum = sem("pT_in_psum")
        pT_ready = sem("pT_ready")
        av_ready = sem("av_ready")
        outT_ready = sem("outT_ready")
        y_in_psum = sem("y_in_psum")
        x_updated = sem("x_updated")
        hidden_in_psum = sem("hidden_in_psum")
        gate_ready = sem("gate_ready")
        hid_ready = sem("hid_ready")
        pool_held = sem("pool_held")
        dve_held = sem("dve_held")
        stored = sem("stored")

        block = ctx.enter_context(nc.Block())

        @block.sync
        def _(sp):
            sp.dma_start(xs[:, :, :], x.rearrange("b s d -> s b d")).then_inc(x_loaded, 16)
            sp.dma_start(norm_sb[:, :, :], norms).then_inc(params_loaded, 16)
            sp.dma_start(hbias[:, :, :], hidden_biases).then_inc(params_loaded, 16)
            sp.dma_start(ctx_sb[:, :], ctxT).then_inc(params_loaded, 16)
            sp.dma_start(obias[:, :, :], out_biases.partition_broadcast(128)).then_inc(params_loaded, 16)

            def load_attention(st, A, cross, thin, layer=None):
                at_least(sp, w_split, A)
                if thin:
                    sp.wait_ge(pad_zeroed, 2 if cross else 1)
                kv_rows = C if cross else D
                if layer is not None:
                    src = deep_w["cross" if cross else "self"]
                    q, k, v, wo = [f(layer) for f in src]
                elif thin:
                    q, k, v, wo = thin_w["cross" if cross else "self"]
                else:
                    q, k, v, wo = attn_w[A]
                width = THIN if thin else SLOT
                for n, (w, rows) in enumerate(((q, D), (k, kv_rows), (v, kv_rows))):
                    dst = w_raw[0:rows, n, :].rearrange("p (h e) -> p h e", e=SLOT)[:, :, 0:width]
                    sp.dma_start(dst, w.rearrange("p (h e) -> p h e", e=width)).then_inc(w_loaded, 16)
                halves = wo.rearrange("(c two e) n -> two e c n", two=2, e=width)
                for two in range(2):
                    sp.dma_start(wo_sb[two * SLOT:two * SLOT + width, int(cross), :, :],
                                 halves[two]).then_inc(w_loaded, 16)

            def load_ff(st, F, gated, A_before, layer=None):
                at_least(sp, w_split, A_before + 1)
                w1, w2 = [f(layer) for f in deep_w["ff"]] if layer is not None else ff_w[F]
                sp.dma_start(w1_raw[:, 0:(2 if gated else 1) * FF], w1).then_inc(ff_loaded, 16)
                sp.dma_start(w2_sb[:, :, :], w2.rearrange("(c p) n -> p c n", p=128)).then_inc(ff_loaded, 16)

            run_network(sp, load_attention, load_ff)
            sp.wait_ge(x_updated, B * STAGES)
            sp.dma_start(out.rearrange("b s d -> s b d"), xs[:, :, :]).then_inc(stored, 16)
            sp.wait_ge(stored, 16)

        @block.gpsimd
        def _(pool):
            nc.gpsimd.memset(half[:, :], -0.5).then_inc(half_ready, 1)
            nc.gpsimd.memset(ident[:, :], 0.0).then_inc(ident_zeroed, 1)
            pool.wait_ge(ident_zeroed, 1)
            nc.gpsimd.affine_select(out=ident[:, :], in_=ident[:, :], compare_op=ALU.not_equal, fill=1.0,
                                    base=0, pattern=[[-1, 128]], channel_multiplier=1).then_inc(ident_ready, 1)
            pool.wait_ge(half_ready, 1)
            pool.wait_ge(params_loaded, 64)

            def zero_padding(A):
                pool.wait_ge(w_split, A + 1)
                nc.gpsimd.memset(w_raw[:, :, :], 0.0)
                nc.gpsimd.memset(wo_sb[:, A - 1, :, :], 0.0).then_inc(pad_zeroed, 1)

            def inverse_deviation(st):
                hold(pool, stats_ready, st + 1, pool_held)
                nc.gpsimd.tensor_scalar(ve[:, :], mv[:, :, 1], EPS, None, ALU.add).then_inc(ve_ready, 1)
                pool.wait_ge(ve_ready, st + 1)
                nc.gpsimd.tensor_tensor(rstd[:, :], ve[:, :], half[:, :], ALU.pow).then_inc(rstd_ready, 1)

            def add_output_bias(st, g):
                hold(pool, xhat_ready, st * NG + g + 1, pool_held)
                rows = xs[:, bass.ds(g * GB, GB), :]
                bias = obias[:, bass.ds(st, 1), :].broadcast_to([128, GB, D])
                nc.gpsimd.tensor_tensor(rows, rows, bias, ALU.add).then_inc(xbias_ready, 1)

            def normalise(Q, q, keys):
                pool.wait_ge(rinv_ready, Q + 1)
                p = probs[:, q % 2, :, 0:keys]
                r = rinv[:, q % 2, :].unsqueeze(2).broadcast_to([128, 4, keys])
                nc.gpsimd.tensor_tensor(p, p, r, ALU.mult).then_inc(probs_ready, 1)

            def attention(st, A, cross, thin, layer=None):
                keys = T if cross else S
                inverse_deviation(st)
                add_output_bias(st, 0)
                add_output_bias(st, 1)
                for q in range(2):
                    normalise(A * 64 + q, q, keys)
                if layer is None and A in (1, 2):
                    zero_padding(A)

                def group(g, more, last):
                    Q = A * 64 + g * QUADS
                    for q in range(1, QUADS + 1):
                        if not last or q + 1 < QUADS:
                            normalise(Q + (q + 1), q + 1, keys)
                    if more:
                        add_output_bias(st, g + 2)

                with pool.Fori(0, NG // 2 - 1) as p:
                    group(p * 2, True, False)
                    group(p * 2 + 1, True, False)
                group(NG - 2, False, False)
                group(NG - 1, False, True)

            def feed_forward(st, F, gated, A_before, layer=None):
                inverse_deviation(st)
                add_output_bias(st, 0)
                add_output_bias(st, 1)
                with pool.Fori(0, NG - 2) as g:
                    add_output_bias(st, g + 2)

            run_network(pool, attention, feed_forward)

        @block.scalar
        def _(act):
            def evacuate_q(n, par, c, scale):
                act.wait_ge(q_in_psum, n + 1)
                nc.scalar.activation(qT[:, par, c, :], qv_ps[:, 0:GN], ACT.Copy, scale=scale).then_inc(q_ready, 1)

            def evacuate_v(n, par, v, keys):
                act.wait_ge(v_in_psum, n + 1)
                nc.scalar.activation(v_sb[0:keys, par, v // 2, (v % 2) * 512:(v % 2) * 512 + 512],
                                     qv_ps[0:keys, :], ACT.Copy).then_inc(v_ready, 1)

            def exponentials(Q, q, keys):
                act.wait_ge(negmax_ready, Q + 1)
                if isinstance(Q, int) and Q < 2:
                    pass
                else:
                    act.wait_ge(pT_in_psum, Q - 1)
                for h in range(4):
                    e = nc.scalar.activation(probs[:, q % 2, h, 0:keys], score_ps[q % 2][:, h, 0:keys], ACT.Exp,
                                             bias=negmax[:, q % 2, h:h + 1], accum_out=sums[:, q % 2, h:h + 1])
                e.then_inc(exp_ready, 1)

            def evacuate_pT(Q, q, keys):
                act.wait_ge(pT_in_psum, Q + 1)
                nc.scalar.activation(pT[0:keys, q % 4, :, :], pT_ps[q % 2][0:keys, :, :], ACT.Copy)\
                    .then_inc(pT_ready, 1)

            def attention(st, A, cross, thin, layer=None):
                keys = T if cross else S
                scale = float(THIN if thin else SLOT) ** -0.5
                for c in range(CH):
                    evacuate_q(A * 64 + c, 0, c, scale)
                for v in range(2 * GB):
                    evacuate_v(A * 32 + v, 0, v, keys)
                for q in range(2):
                    exponentials(A * 64 + q, q, keys)
                evacuate_pT(A * 64, 0, keys)

                def group(g, par, last):
                    Q = A * 64 + g * QUADS
                    for q in range(1, QUADS + 1):
                        if not last or q + 1 < QUADS:
                            exponentials(Q + (q + 1), q + 1, keys)
                        if not last:
                            for c in QK_AT.get(q, ()):
                                evacuate_q(A * 64 + (g + 1) * CH + c, 1 - par, c, scale)
                            if q in V_AT:
                                evacuate_v(A * 32 + (g + 1) * 4 + V_AT[q], 1 - par, V_AT[q], keys)
                        if not last or q < QUADS:
                            evacuate_pT(Q + q, q, keys)

                with act.Fori(0, NG // 2 - 1) as p:
                    group(p * 2, 0, False)
                    group(p * 2 + 1, 1, False)
                group(NG - 2, 0, False)
                group(NG - 1, 1, True)

            def feed_forward(st, F, gated, A_before, layer=None):
                nc.scalar.activation(hb[:, :], hbias[:, bass.ds(F, 1), :].rearrange("p a b -> p (a b)"), ACT.Copy)\
                    .then_inc(hb_ready, 1)
                act.wait_ge(hb_ready, F + 1)

                def activate(g, par):
                    for c in range(FC):
                        n = F * 32 + g * FC + c
                        act.wait_ge(hidden_in_psum, n + 1)
                        b = FC + c if gated else c
                        bias = hb[:, b:b + 1]
                        dst = gate[:, c % 2, :] if gated else hid[:, par, c, :]
                        nc.scalar.activation(dst, score_ps[c % 2][:, :, :].rearrange("p a b -> p (a b)")[:, 0:GN],
                                             ACT.Gelu, bias=bias).then_inc(gate_ready if gated else hid_ready, 1)

                with act.Fori(0, NG // 2) as p:
                    activate(p * 2, 0)
                    activate(p * 2 + 1, 1)

            act.wait_ge(params_loaded, 64)
            run_network(act, attention, feed_forward)

        @block.vector
        def _(dve):
            def statistics(b, n, src, keep=None):
                nc.vector.bn_stats(bnst[:, :], src).then_inc(bn_ready, 1)
                if keep is not None:
                    keep()
                hold(dve, bn_ready, n + 1, dve_held)
                nc.vector.bn_aggr(mv_row[:, :], bnst[:, :]).then_inc(aggr_ready, 1)
                hold(dve, aggr_ready, n + 1, dve_held)
                return nc.vector.tensor_copy(mv[:, bass.ds(b, 1), :].rearrange("p a d -> p (a d)"), mv_row[:, :])

            def split_weights(raw, hi, lo, hi_ready, split, n):
                nc.vector.tensor_copy(hi, raw).then_inc(hi_ready, 1)
                dve.wait_ge(hi_ready, n + 1)
                return nc.vector.tensor_tensor(lo, raw, hi, ALU.subtract)

            def normalise_rows(st, g):
                if isinstance(g, int) and g == 0:
                    dve.wait_ge(rstd_ready, st + 1)
                for i in range(GB):
                    b = g * GB + i
                    op = nc.vector.tensor_scalar(
                        xhat[:, i, :], xs[:, bass.ds(b, 1), :].rearrange("p a d -> p (a d)"),
                        mv[:, bass.ds(b, 1), 0:1].rearrange("p a d -> p (a d)"),
                        rstd[:, bass.ds(b, 1)], ALU.subtract, ALU.mult)
                op.then_inc(xhat_ready, 1)

            def take_hT(st, g, cross=False):
                N = st * NG + g
                dve.wait_ge(hT_in_psum, N + 1)
                gain = norm_sb[:, bass.ds(st, 1), 0:1].rearrange("p a d -> p (a d)")
                shift = norm_sb[:, bass.ds(st, 1), 1:2].rearrange("p a d -> p (a d)")
                nc.vector.tensor_scalar(hT[:, :], k_ps[:, 0:GN], gain, shift, ALU.mult, ALU.add)\
                    .then_inc(hT_affine, 1)
                if cross:
                    src = ctx_sb[:, bass.ds(g * (GB * T), GB * T)]
                    nc.vector.tensor_copy(c_hi[:, :], src)
                dve.wait_ge(hT_affine, N + 1)
                nc.vector.tensor_copy(h_hi[:, :], hT[:, :]).then_inc(h_hi_ready, 1)
                dve.wait_ge(h_hi_ready, N + 1)
                if cross:
                    nc.vector.tensor_tensor(c_lo[:, :], src, c_hi[:, :], ALU.subtract)
                nc.vector.tensor_tensor(h_lo[:, :], hT[:, :], h_hi[:, :], ALU.subtract).then_inc(hT_ready, 1)

            def update_x(st, b, y, with_stats_done):
                n = st * B + b
                dve.wait_ge(y_in_psum, n + 1)
                row = xs[:, bass.ds(b, 1), :].rearrange("p a d -> p (a d)")
                nc.vector.tensor_tensor(x_row[:, :], y[:, 0:D], row, ALU.add).then_inc(y_taken, 1)
                dve.wait_ge(y_taken, n + 2)

                def keep():
                    nc.vector.tensor_copy(row, x_row[:, :]).then_inc(x_updated, 1)

                op = statistics(b, n + B, x_row[:, :], keep)
                if with_stats_done:
                    op.then_inc(stats_ready, 1)

            def row_max(Q, q, keys):
                dve.wait_ge(scores_ready, Q + 1)
                nc.vector.tensor_reduce(negmax[:, q % 2, :], score_ps[q % 2][:, :, 0:keys], AX.X, ALU.max,
                                        negate=True).then_inc(negmax_ready, 1)

            def inverse_sum(Q, q):
                dve.wait_ge(exp_ready, Q + 1)
                nc.vector.reciprocal(rinv[:, q % 2, :], sums[:, q % 2, :]).then_inc(rinv_ready, 1)

            def evacuate_k(n, par, c, keys):
                dve.wait_ge(k_in_psum, n + 1)
                nc.vector.tensor_copy(kT[:, par, c, 0:GB * keys], k_ps[:, 0:GB * keys]).then_inc(k_ready, 1)

            def evacuate_out(n, m):
                dve.wait_ge(av_ready, n + 1)
                nc.vector.tensor_copy(outT[:, m // 2, 4 * (m % 2):4 * (m % 2) + 4, :],
                                      o_ps[:, :].rearrange("p (c s) -> p c s", c=4)).then_inc(outT_ready, 1)

            def attention(st, A, cross, thin, layer=None):
                keys = T if cross else S
                rows = C if cross else D
                dve.wait_ge(w_loaded, (A + 1) * (16 * W_DMAS))
                split_weights(w_raw[:, 0, :], w_hi[:, 0, :], w_lo[:, 0, :], w_hi_ready, w_split, A * 2)
                split_weights(w_raw[0:rows, 1:3, :], w_hi[0:rows, 1:3, :], w_lo[0:rows, 1:3, :],
                              w_hi_ready, w_split, A * 2 + 1).then_inc(w_split, 1)
                normalise_rows(st, 0)
                take_hT(st, 0, cross)
                normalise_rows(st, 1)
                for c in range(CH):
                    evacuate_k(A * 64 + c, 0, c, keys)
                take_hT(st, 1, cross)
                row_max(A * 64, 0, keys)
                row_max(A * 64 + 1, 1, keys)
                inverse_sum(A * 64, 0)
                row_max(A * 64 + 2, 2, keys)
                inverse_sum(A * 64 + 1, 1)

                def group(g, par, more, last):
                    Q = A * 64 + g * QUADS
                    for q in range(1, QUADS + 1):
                        if not last or q + 2 < QUADS:
                            row_max(Q + (q + 2), q + 2, keys)
                        if q % 2 == 0:
                            evacuate_out(A * 32 + g * 4 + (q // 2 - 1), q // 2 - 1)
                        if not last:
                            for c in QK_AT.get(q, ()):
                                evacuate_k(A * 64 + (g + 1) * CH + c, 1 - par, c, keys)
                        if not last or q + 1 < QUADS:
                            inverse_sum(Q + (q + 1), q + 1)
                        if more and q == 6:
                            normalise_rows(st, g + 2)
                        if more and q == QUADS:
                            take_hT(st, g + 2, cross)
                        if q == OUT_AT[0]:
                            dve.wait_ge(xbias_ready, st * NG + g + 1)
                        if q in OUT_AT:
                            i = OUT_AT.index(q)
                            update_x(st, g * GB + i, y_ps, last and i == 1)

                with dve.Fori(0, NG // 2 - 1) as p:
                    group(p * 2, 0, True, False)
                    group(p * 2 + 1, 1, True, False)
                group(NG - 2, 0, False, False)
                group(NG - 1, 1, False, True)

            def feed_forward(st, F, gated, A_before, layer=None):
                wide = (2 if gated else 1) * FF
                dve.wait_ge(ff_loaded, (F + 1) * (16 * FF_DMAS))
                split_weights(w1_raw[:, 0:wide], w1_hi[:, 0:wide], w1_lo[:, 0:wide], w1_hi_ready, w1_split, F)\
                    .then_inc(w1_split, 1)

                def gated_product(g, par):
                    for c in range(FC if gated else 0):
                        n = F * 32 + g * FC + c
                        dve.wait_ge(gate_ready, (0 if F == 0 else 32) + g * FC + c + 1)
                        bias = hbias[:, bass.ds(F, 1), c:c + 1].rearrange("p a b -> p (a b)")
                        nc.vector.scalar_tensor_tensor(
                            hid[:, par, c, :], pT_ps[c % 2][:, :, :].rearrange("p a b -> p (a b)")[:, 0:GN],
                            bias, gate[:, c % 2, :], ALU.add, ALU.mult).then_inc(hid_ready, 1)

                normalise_rows(st, 0)
                take_hT(st, 0)
                normalise_rows(st, 1)
                gated_product(0, 0)
                take_hT(st, 1)

                def group(g, par, more, last):
                    if more:
                        normalise_rows(st, g + 2)
                    if not last:
                        gated_product(g + 1, 1 - par)
                    if more:
                        take_hT(st, g + 2)
                    dve.wait_ge(xbias_ready, st * NG + g + 1)
                    update_x(st, g * GB, y_ps, False)
                    update_x(st, g * GB + 1, o_ps, last)

                with dve.Fori(0, NG // 2 - 1) as p:
                    group(p * 2, 0, True, False)
                    group(p * 2 + 1, 1, True, False)
                group(NG - 2, 0, False, False)
                group(NG - 1, 1, False, True)

            dve.sem_inc(outT_ready, 1)
            dve.sem_inc(y_taken, 1)
            dve.wait_ge(x_loaded, 16)
            for b in range(B):
                op = statistics(b, b, xs[:, b, :])
            op.then_inc(stats_ready, 1)
            dve.wait_ge(params_loaded, 64)
            dve.wait_ge(stats_ready, 1)

            run_network(dve, attention, feed_forward)

        @block.tensor
        def _(pe):
            pe.wait_ge(ident_ready, 1)

            def transpose_rows(st, g, k_before):
                N = st * NG + g
                pe.wait_ge(xhat_ready, N + 1)
                at_least(pe, k_ready, k_before)
                at_least(pe, hT_ready, N)
                for i in range(GB):
                    m = nc.tensor.transpose(k_ps[:, i * S:(i + 1) * S], xhat[:, i, :], ident[:, :])
                m.then_inc(hT_in_psum, 1)

            def three_passes(dst, l_hi, l_lo, r_hi, r_lo):
                nc.tensor.matmul(dst, l_hi, r_lo, start=True, stop=False)
                nc.tensor.matmul(dst, l_lo, r_hi, start=False, stop=False)
                return nc.tensor.matmul(dst, l_hi, r_hi, start=False, stop=True)

            def project_qk(A, g, c, cross, v_before):
                n = A * 64 + g * CH + c
                cols = slice(c * 128, c * 128 + 128)
                at_least(pe, q_ready, n)
                at_least(pe, v_ready, v_before)
                three_passes(qv_ps[:, 0:GN], w_hi[:, 0, cols], w_lo[:, 0, cols], h_hi[:, :], h_lo[:, :])\
                    .then_inc(q_in_psum, 1)
                at_least(pe, k_ready, n)
                rows, keys = (C, T) if cross else (D, S)
                s_hi, s_lo = (c_hi, c_lo) if cross else (h_hi, h_lo)
                three_passes(k_ps[:, 0:GB * keys], w_hi[0:rows, 1, cols], w_lo[0:rows, 1, cols],
                             s_hi[:, :], s_lo[:, :]).then_inc(k_in_psum, 1)

            def project_v(A, g, v, cross, q_before):
                n = A * 32 + g * 4 + v
                rows, keys = (C, T) if cross else (D, S)
                s_hi, s_lo = (c_hi, c_lo) if cross else (h_hi, h_lo)
                i, cols = v // 2, slice((v % 2) * 512, (v % 2) * 512 + 512)
                at_least(pe, v_ready, n)
                at_least(pe, q_ready, q_before)
                three_passes(qv_ps[0:keys, :], s_hi[:, i * keys:(i + 1) * keys], s_lo[:, i * keys:(i + 1) * keys],
                             w_hi[0:rows, 2, cols], w_lo[0:rows, 2, cols]).then_inc(v_in_psum, 1)

            def scores(Q, q, par, keys):
                if not isinstance(Q, int) or Q >= 2:
                    pe.wait_ge(exp_ready, Q - 1)
                i, j = (q // 4) % GB, q % 4
                lo = SLOT * (q % 2)
                for h in range(4):
                    c = 4 * (j // 2) + h
                    m = nc.tensor.matmul(score_ps[q % 2][:, h, 0:keys],
                                         qT[lo:lo + SLOT, par, c, i * S:(i + 1) * S],
                                         kT[lo:lo + SLOT, par, c, i * keys:(i + 1) * keys], start=True, stop=True)
                m.then_inc(scores_ready, 1)

            def transpose_probs(Q, q, keys):
                pe.wait_ge(probs_ready, Q + 1)
                for h in range(4):
                    m = nc.tensor.transpose(pT_ps[q % 2][0:keys, h, :], probs[:, q % 2, h, 0:keys], ident[:, :])
                m.then_inc(pT_in_psum, 1)

            def weigh_values(Q, n, q, par, keys):
                pe.wait_ge(pT_ready, Q + 2)
                pe.wait_ge(outT_ready, n + 1)
                for h in range(4):
                    for odd in range(2):
                        head = 2 * (4 * ((q % 4) // 2) + h) + odd
                        m = nc.tensor.matmul(o_ps[odd * SLOT:(odd + 1) * SLOT, h * S:(h + 1) * S],
                                             v_sb[0:keys, par, q // 4, head * SLOT:(head + 1) * SLOT],
                                             pT[0:keys, (q + odd) % 4, h, :], start=True, stop=True)
                m.then_inc(av_ready, 1)

            def project_out(st, b, pairs_done, slot, cross):
                pe.wait_ge(outT_ready, pairs_done + 1)
                pe.wait_ge(y_taken, st * B + b + 1)
                for c in range(CH):
                    m = nc.tensor.matmul(y_ps[:, 0:D], outT[:, slot, c, :], wo_sb[:, int(cross), c, :],
                                         start=(c == 0), stop=(c == CH - 1))
                m.then_inc(y_in_psum, 1)

            def attention(st, A, cross, thin, layer=None):
                keys = T if cross else S
                k0, v0 = A * 64, A * 32
                pe.wait_ge(w_split, A + 1)
                pe.wait_ge(w_loaded, (A + 1) * (16 * W_DMAS))
                transpose_rows(st, 0, k0)
                pe.wait_ge(hT_ready, st * NG + 1)
                for c in range(CH):
                    project_qk(A, 0, c, cross, v0)
                for v in range(2 * GB):
                    project_v(A, 0, v, cross, k0 + CH)
                transpose_rows(st, 1, k0 + CH)
                pe.wait_ge(q_ready, k0 + CH)
                pe.wait_ge(k_ready, k0 + CH)
                for q in range(3):
                    scores(A * 64 + q, q, 0, keys)
                pe.wait_ge(hT_ready, st * NG + 2)
                transpose_probs(A * 64, 0, keys)

                def group(g, par, more, last):
                    Q = A * 64 + g * QUADS
                    n = A * 32 + g * 4
                    for q in range(1, QUADS + 1):
                        if q == 1:
                            pe.wait_ge(v_ready, v0 + g * 4 + 4)
                            if not last:
                                pe.wait_ge(hT_ready, st * NG + g + 2)
                        if q in (QUADS - 2, QUADS) and not last:
                            pe.wait_ge(q_ready, k0 + (g + 1) * CH + (4 if q < QUADS else CH))
                            pe.wait_ge(k_ready, k0 + (g + 1) * CH + (4 if q < QUADS else CH))
                        if not last or q + 2 < QUADS:
                            ahead = q + 2 >= QUADS
                            scores(Q + (q + 2), q + 2, 1 - par if ahead else par, keys)
                        if q % 2 == 0:
                            weigh_values(Q + (q - 2), n + (q // 2 - 1), q - 2, par, keys)
                        if not last:
                            for c in QK_AT.get(q, ()):
                                v_done = sum(1 for s in V_AT if s < q)
                                project_qk(A, g + 1, c, cross, v0 + (g + 1) * 4 + v_done)
                            if q in V_AT:
                                q_done = sum(len(cs) for s, cs in QK_AT.items() if s <= q)
                                project_v(A, g + 1, V_AT[q], cross, k0 + (g + 1) * CH + q_done)
                        if more and q == QUADS:
                            transpose_rows(st, g + 2, k0 + (g + 2) * CH)
                        if not last or q < QUADS:
                            transpose_probs(Q + q, q, keys)
                        if q in OUT_AT:
                            i = OUT_AT.index(q)
                            project_out(st, g * GB + i, n + 2 * (i + 1), i, cross)

                with pe.Fori(0, NG // 2 - 1) as p:
                    group(p * 2, 0, True, False)
                    group(p * 2 + 1, 1, True, False)
                group(NG - 2, 0, False, False)
                group(NG - 1, 1, False, True)

            def feed_forward(st, F, gated, A_before, layer=None):
                k0 = (A_before + 1) * 64
                pe.wait_ge(w1_split, F + 1)
                pe.wait_ge(ff_loaded, (F + 1) * (16 * FF_DMAS))

                def flat(bank):
                    return bank[:, :, :].rearrange("p a b -> p (a b)")[:, 0:GN]

                def hidden(g):
                    pe.wait_ge(hT_ready, st * NG + g + 1)
                    for c in range(FC):
                        n = F * 32 + g * FC + c
                        if not isinstance(n, int) or n >= 2:
                            pe.wait_ge(hid_ready, n - 1)
                        if gated:
                            cols = slice(c * 128, c * 128 + 128)
                            three_passes(flat(pT_ps[c % 2]), w1_hi[:, cols], w1_lo[:, cols], h_hi[:, :], h_lo[:, :])
                        b = FC + c if gated else c
                        cols = slice(b * 128, b * 128 + 128)
                        three_passes(flat(score_ps[c % 2]), w1_hi[:, cols], w1_lo[:, cols], h_hi[:, :], h_lo[:, :])\
                            .then_inc(hidden_in_psum, 1)

                def second(g, par):
                    pe.wait_ge(hid_ready, F * 32 + g * FC + FC)
                    for i, y in enumerate((y_ps, o_ps)):
                        pe.wait_ge(y_taken, st * B + g * GB + 1)
                        for c in range(FC):
                            m = nc.tensor.matmul(y[:, 0:D], hid[:, par, c, i * S:(i + 1) * S], w2_sb[:, c, :],
                                                 start=(c == 0), stop=(c == FC - 1))
                        m.then_inc(y_in_psum, 1)

                def group(g, par, more, last):
                    if not last:
                        hidden(g + 1)
                    if more:
                        transpose_rows(st, g + 2, k0)
                    second(g, par)

                transpose_rows(st, 0, k0)
                hidden(0)
                transpose_rows(st, 1, k0)
                with pe.Fori(0, NG // 2 - 1) as p:
                    group(p * 2, 0, True, False)
                    group(p * 2 + 1, 1, True, False)
                group(NG - 2, 0, False, False)
                group(NG - 1, 1, False, True)

            run_network(pe, attention, feed_forward)


def kernel(**inputs):
    import numpy as np
    from concourse.bacc import Bacc
    from concourse.bass_utils import run_bass_kernel_spmd

    nc = Bacc("TRN2", target_bir_lowering=False, num_devices=1)
    arrays = {}

    def dram(name, a):
        a = np.ascontiguousarray(a)
        arrays[name] = a
        return nc.dram_tensor(name, a.shape, mybir.dt.from_np(a.dtype), kind="ExternalInput").ap()

    def given(name):
        return dram(name, inputs[name])

    L0, L1, L2, L3 = (f"L{i}_xattn_" for i in range(4))
    pairs = [(L0 + "ln1_g", L0 + "ln1_b"), (L0 + "ln2_g", L0 + "ln2_b"), (L0 + "ln3_g", L0 + "ln3_b"),
             (L1 + "n1_g", L1 + "n1_b"), (L1 + "n2_g", L1 + "n2_b"), (L1 + "n3_g", L1 + "n3_b"),
             (L1 + "n4_g", L1 + "n4_b"),
             (L2 + "g1", L2 + "be1"), (L2 + "g2", L2 + "be2"), (L2 + "g3", L2 + "be3")]
    biases = [L0 + "sa_bo", L0 + "ca_bo", L0 + "ff_b2", L1 + "so_b", L1 + "f1_b2", L1 + "co_b", L1 + "f2_b2",
              L2 + "bo1", L2 + "bo2", L2 + "b2"]
    gains = [np.asarray(inputs[g]) for g, _ in pairs]
    shifts = [np.asarray(inputs[b]) for _, b in pairs]
    rows = [np.asarray(inputs[b]) for b in biases]
    for i in range(DEPTH3):
        for n, b in (("ln1", "b_sa_o"), ("ln2", "b_ca_o"), ("ln3", "b_ff2")):
            gains.append(np.asarray(inputs[f"{L3}{n}_g"])[i])
            shifts.append(np.asarray(inputs[f"{L3}{n}_b"])[i])
            rows.append(np.asarray(inputs[L3 + b])[i])
    norms = dram("norms", np.stack([np.stack(gains, 1), np.stack(shifts, 1)], 2))
    out_biases = dram("out_biases", np.stack(rows))
    hidden = []
    for b in (inputs[L0 + "ff_b1"], inputs[L1 + "f1_b1"], inputs[L1 + "f2_b1"], inputs[L2 + "bp"],
              *np.asarray(inputs[L3 + "b_ff1"])):
        h = np.zeros((128, 2 * FC), np.float32)
        h[:, :len(b) // 128] = np.asarray(b).reshape(-1, 128).T
        hidden.append(h)
    hidden_biases = dram("hidden_biases", np.stack(hidden, 1))
    ctxT = dram("ctxT", np.asarray(inputs["ctx_768"]).transpose(2, 0, 1).reshape(C, B * T))

    attn_w = {
        0: [given(L0 + n) for n in ("sa_wq", "sa_wk", "sa_wv", "sa_wo")],
        1: [given(L0 + n) for n in ("ca_wq", "ca_wk", "ca_wv", "ca_wo")],
        4: [given(L2 + n) for n in ("Wq1", "Wk1", "Wv1", "Wo1")],
        5: [given(L2 + n) for n in ("Wq2", "Wk2", "Wv2", "Wo2")],
    }
    thin_w = {"self": [given(L1 + n) for n in ("sq_w", "sk_w", "sv_w", "so_w")],
              "cross": [given(L1 + n) for n in ("cq_w", "ck_w", "cv_w", "co_w")]}
    ff_w = {0: (given(L0 + "ff_w1"), given(L0 + "ff_w2")), 1: (given(L1 + "f1_w1"), given(L1 + "f1_w2")),
            2: (given(L1 + "f2_w1"), given(L1 + "f2_w2")), 3: (given(L2 + "Wp"), given(L2 + "W2"))}
    qkv, sao, wq, kv, cao, ff1, ff2 = (given(L3 + n) for n in
                                       ("w_qkv", "w_sa_o", "w_q", "w_kv", "w_ca_o", "w_ff1", "w_ff2"))

    def of_layer(w, lo=None, hi=None):
        cols = slice(0, w.shape[2]) if lo is None else slice(lo, hi)
        return lambda layer: w[bass.ds(layer, 1), :, cols].rearrange("a p n -> (a p) n")

    deep_w = {
        "self": [of_layer(qkv, 0, INNER), of_layer(qkv, INNER, 2 * INNER), of_layer(qkv, 2 * INNER, 3 * INNER),
                 of_layer(sao)],
        "cross": [of_layer(wq), of_layer(kv, 0, INNER), of_layer(kv, INNER, 2 * INNER), of_layer(cao)],
        "ff": [of_layer(ff1), of_layer(ff2)],
    }
    out = nc.dram_tensor("out", (B, S, D), F32, kind="ExternalOutput").ap()
    build(nc, given("x"), ctxT, norms, out_biases, hidden_biases, attn_w, thin_w, ff_w, deep_w, out)
    r = run_bass_kernel_spmd(nc, [arrays], core_ids=[0])
    return r.results[0]["out"]
```

```python
from contextlib import ExitStack

import concourse.bass as bass
from concourse import mybir

F32 = mybir.dt.float32
F32R = mybir.dt.float32r
ALU = mybir.AluOpType
ACT = mybir.ActivationFunctionType
AX = mybir.AxisListType

B, S, D = 16, 128, 128
T, C = 120, 96
HEADS, SLOT = 16, 64
INNER = HEADS * SLOT
THIN = 8
FF = 4 * D
EPS = 1e-5

GB = 2
NG = B // GB
GN = GB * S
QUADS = GB * 4
CH = INNER // 128
FC = FF // 128
DEPTH3 = 4
STAGES, ATTNS, FFS = 10 + 3 * DEPTH3, 6 + 2 * DEPTH3, 4 + DEPTH3

QK_AT = {1: (0, 1), 2: (2,), 3: (3, 4), 6: (5,), 7: (6, 7)}
V_AT = {1: 0, 3: 1, 4: 2, 7: 3}
OUT_AT = (5, 8)
QKV_DMAS, WO_DMAS, FF_DMAS = 3, 2, 2
W_PARTS = 6


class Attention:

    def __init__(self, stage, number, cross=False, thin=False, layer=None):
        self.stage, self.number, self.cross, self.thin, self.layer = stage, number, cross, thin, layer
        self.keys, self.rows = (T, C) if cross else (S, D)
        self.slot = int(cross)
        self.turn = number // 2 if isinstance(number, int) else layer + 3
        self.scale = float(THIN if thin else SLOT) ** -0.5


class FeedForward:

    def __init__(self, stage, number, gated=False, layer=None, before=None):
        self.stage, self.number, self.gated, self.layer = stage, number, gated, layer
        self.attentions = before


def deep_layer(layer):
    return [Attention(layer * 3 + 10, layer * 2 + 6, layer=layer),
            Attention(layer * 3 + 11, layer * 2 + 7, cross=True, layer=layer),
            FeedForward(layer * 3 + 12, layer + 4, layer=layer, before=layer * 2 + 8)]


FRONT = [Attention(0, 0), Attention(1, 1, cross=True), FeedForward(2, 0, gated=True, before=2),
         Attention(3, 2, thin=True), FeedForward(4, 1, before=3), Attention(5, 3, cross=True, thin=True),
         FeedForward(6, 2, before=4),
         Attention(7, 4), Attention(8, 5, cross=True), FeedForward(9, 3, gated=True, before=6)]


def run_network(eng, run):
    def run_list(stages, following, first):
        after = first
        for stage, nxt in zip(stages, stages[1:] + [following]):
            run(stage, nxt, after)
            after = isinstance(stage, Attention)

    run_list(FRONT, deep_layer(0)[0], None)
    with eng.Fori(0, DEPTH3 - 1) as layer:
        run_list(deep_layer(layer), deep_layer(layer + 1)[0], False)
    run_list(deep_layer(DEPTH3 - 1), None, False)


def is_cross(stage):
    return isinstance(stage, Attention) and stage.cross


def next_attention(a, nxt):
    if isinstance(nxt, Attention):
        return nxt
    if a.layer is not None:
        return None if isinstance(a.layer, int) else Attention(a.stage + 2, a.number + 1, layer=a.layer + 1)
    later = [s for s in FRONT if isinstance(s, Attention) and s.number == a.number + 1]
    return later[0] if later else deep_layer(0)[0]


def at_least(eng, sem, value):
    if isinstance(value, int) and value <= 0:
        return
    eng.wait_ge(sem, value)


def hold(eng, sem, value, held):
    eng.wait_ge(sem, value)
    eng.sem_inc(held, 1)


def build(nc, x, ctxT, norms, out_biases, hidden_biases, attn_w, thin_w, ff_w, deep_w, out):
    with ExitStack() as ctx:
        def sb(name, shape, dt=F32):
            return ctx.enter_context(nc.sbuf_tensor(name, shape, dt))

        def psum(name, shape):
            return ctx.enter_context(nc.psum_tensor(name, shape, F32))

        def sem(name):
            return ctx.enter_context(nc.semaphore(name))

        xs = sb("xs", [128, B, D])
        ctx_sb = sb("ctx_sb", [C, B * T])
        norm_sb = sb("norm_sb", [128, STAGES, 2])
        obias = sb("obias", [128, STAGES, D])
        hbias = sb("hbias", [128, FFS, 2 * FC])
        ident = sb("ident", [128, 128])
        eps = sb("eps", [128, 2 * GB])
        half = sb("half", [128, 2 * GB])
        bnst = sb("bnst", [128, 6])
        mv_row = sb("mv_row", [128, 2])
        x_row = sb("x_row", [128, D])
        mv = sb("mv", [128, B, 2])
        ve = sb("ve", [128, 2 * GB])
        rstd = sb("rstd", [128, B])
        xhat = sb("xhat", [128, GB, D])
        hT = sb("hT", [128, GN])
        h_hi = sb("h_hi", [128, GN], F32R)
        h_lo = sb("h_lo", [128, GN], F32R)
        c_hi = sb("c_hi", [C, GB * T], F32R)
        c_lo = sb("c_lo", [C, GB * T], F32R)
        w_raw = sb("w_raw", [128, 3, INNER])
        w_hi = sb("w_hi", [128, 2, 3, INNER], F32R)
        w_lo = sb("w_lo", [128, 2, 3, INNER], F32R)
        wo_sb = sb("wo_sb", [128, 2, CH, D])
        w1_raw = sb("w1_raw", [128, 2 * FF])
        w1_hi = sb("w1_hi", [128, 2 * FF], F32R)
        w1_lo = sb("w1_lo", [128, 2 * FF], F32R)
        w2_sb = sb("w2_sb", [128, FC, D])
        qT = sb("qT", [128, 2, CH, GN])
        kT = sb("kT", [128, 2, CH, GN])
        v_sb = sb("v_sb", [128, 2, GB, INNER])
        negmax = sb("negmax", [128, 2, 4])
        sums = sb("sums", [128, 2, 4])
        rinv = sb("rinv", [128, 2, 4])
        probs = sb("probs", [128, 2, 4, S])
        pT = sb("pT", [128, 4, 4, S])
        outT = sb("outT", [128, 2, CH, S])
        hb = sb("hb", [128, 2 * FC])
        gate = sb("gate", [128, 2, GN])
        hid = sb("hid", [128, 2, FC, GN])

        score_ps = [psum(f"score_ps{i}", [128, 4, 128]) for i in range(2)]
        pT_ps = [psum(f"pT_ps{i}", [128, 4, 128]) for i in range(2)]
        o_ps = psum("o_ps", [128, 512])
        y_ps = psum("y_ps", [128, 512])
        q_ps = psum("q_ps", [128, 512])
        k_ps = psum("k_ps", [128, 512])

        x_loaded = sem("x_loaded")
        params_loaded = sem("params_loaded")
        w_loaded = sem("w_loaded")
        wo_loaded = [sem(f"wo{i}_loaded") for i in range(2)]
        wo_zeroed = sem("wo_zeroed")
        ff_loaded = sem("ff_loaded")
        pad_zeroed = sem("pad_zeroed")
        ident_zeroed = sem("ident_zeroed")
        ident_ready = sem("ident_ready")
        half_ready = sem("half_ready")
        w_hi_ready = sem("w_hi_ready")
        w_split = sem("w_split")
        w1_hi_ready = sem("w1_hi_ready")
        w1_split = sem("w1_split")
        bn_ready = sem("bn_ready")
        aggr_ready = sem("aggr_ready")
        y_taken = sem("y_taken")
        hb_ready = sem("hb_ready")
        stats_ready = sem("stats_ready")
        ve_ready = sem("ve_ready")
        rstd_ready = sem("rstd_ready")
        xhat_ready = sem("xhat_ready")
        xbias_ready = sem("xbias_ready")
        hT_in_psum = sem("hT_in_psum")
        hT_affine = sem("hT_affine")
        h_hi_ready = sem("h_hi_ready")
        hT_ready = sem("hT_ready")
        q_in_psum = sem("q_in_psum")
        k_in_psum = sem("k_in_psum")
        v_in_psum = sem("v_in_psum")
        q_ready = sem("q_ready")
        k_ready = sem("k_ready")
        v_ready = sem("v_ready")
        scores_ready = sem("scores_ready")
        negmax_ready = sem("negmax_ready")
        exp_ready = sem("exp_ready")
        rinv_ready = sem("rinv_ready")
        probs_ready = sem("probs_ready")
        pT_in_psum = sem("pT_in_psum")
        pT_ready = sem("pT_ready")
        av_ready = sem("av_ready")
        outT_ready = sem("outT_ready")
        y_in_psum = sem("y_in_psum")
        x_updated = sem("x_updated")
        hidden_in_psum = sem("hidden_in_psum")
        gate_ready = sem("gate_ready")
        hid_ready = sem("hid_ready")
        pool_held = sem("pool_held")
        dve_held = sem("dve_held")
        stored = sem("stored")

        block = ctx.enter_context(nc.Block())

        @block.sync
        def _(sp):
            sp.dma_start(xs[:, :, :], x.rearrange("b s d -> s b d")).then_inc(x_loaded, 16)
            sp.dma_start(norm_sb[:, :, :], norms).then_inc(params_loaded, 16)
            sp.dma_start(hbias[:, :, :], hidden_biases).then_inc(params_loaded, 16)
            sp.dma_start(ctx_sb[:, :], ctxT).then_inc(params_loaded, 16)
            sp.dma_start(obias[:, :, :], out_biases.partition_broadcast(128)).then_inc(params_loaded, 16)

            def load_attention(a):
                at_least(sp, w_split, a.number * W_PARTS)
                if a.thin:
                    sp.wait_ge(pad_zeroed, 1 + a.slot)
                if a.layer is not None:
                    q, k, v, wo = [f(a.layer) for f in deep_w["cross" if a.cross else "self"]]
                elif a.thin:
                    q, k, v, wo = thin_w["cross" if a.cross else "self"]
                else:
                    q, k, v, wo = attn_w[a.number]
                width = THIN if a.thin else SLOT
                for n, (w, rows) in enumerate(((q, D), (k, a.rows), (v, a.rows))):
                    dst = w_raw[0:rows, n, :].rearrange("p (h e) -> p h e", e=SLOT)[:, :, 0:width]
                    sp.dma_start(dst, w.rearrange("p (h e) -> p h e", e=width)).then_inc(w_loaded, 16)
                return wo, width

            def load_wo(a, wo, width, stages_done):
                at_least(sp, x_updated, stages_done * B)
                if a.thin:
                    sp.wait_ge(wo_zeroed, 1 + a.slot)
                halves = wo.rearrange("(c two e) n -> two e c n", two=2, e=width)
                for two in range(2):
                    sp.dma_start(wo_sb[two * SLOT:two * SLOT + width, a.slot, :, :],
                                 halves[two]).then_inc(wo_loaded[a.slot], 16)

            def load_ff(f, stages_done):
                at_least(sp, x_updated, stages_done * B)
                w1, w2 = [w(f.layer) for w in deep_w["ff"]] if f.layer is not None else ff_w[f.number]
                sp.dma_start(w1_raw[:, 0:(2 if f.gated else 1) * FF], w1).then_inc(ff_loaded, 16)
                sp.dma_start(w2_sb[:, :, :], w2.rearrange("(c p) n -> p c n", p=128)).then_inc(ff_loaded, 16)

            def load(stage, nxt, after_attention):
                if isinstance(stage, Attention):
                    wo, width = load_attention(stage)
                    load_wo(stage, wo, width, wo_free_after(stage))
                else:
                    load_ff(stage, ff_free_after(stage))

            def wo_free_after(a):
                if a.layer is not None:
                    return a.stage - 2 if a.cross else (a.stage - 2)
                return {0: 0, 1: 0, 2: 1, 3: 2, 4: 4, 5: 6}[a.number]

            def ff_free_after(f):
                if f.layer is not None:
                    return f.stage - 2
                return {0: 0, 1: 3, 2: 5, 3: 7}[f.number]

            run_network(sp, load)
            sp.wait_ge(x_updated, B * STAGES)
            sp.dma_start(out.rearrange("b s d -> s b d"), xs[:, :, :]).then_inc(stored, 16)
            sp.wait_ge(stored, 16)

        @block.gpsimd
        def _(pool):
            nc.gpsimd.memset(eps[:, :], EPS).then_inc(half_ready, 1)
            nc.gpsimd.memset(half[:, :], -0.5).then_inc(half_ready, 1)
            nc.gpsimd.memset(ident[:, :], 0.0).then_inc(ident_zeroed, 1)
            pool.wait_ge(ident_zeroed, 1)
            nc.gpsimd.affine_select(out=ident[:, :], in_=ident[:, :], compare_op=ALU.not_equal, fill=1.0,
                                    base=0, pattern=[[-1, 128]], channel_multiplier=1).then_inc(ident_ready, 1)
            pool.wait_ge(half_ready, 2)
            pool.wait_ge(params_loaded, 64)

            def zero_qkv(a):
                pool.wait_ge(w_split, a.number * W_PARTS)
                nc.gpsimd.memset(w_raw[:, :, :], 0.0).then_inc(pad_zeroed, 1)

            def zero_wo(a, stages_done):
                pool.wait_ge(x_updated, stages_done * B)
                nc.gpsimd.memset(wo_sb[:, a.slot, :, :], 0.0).then_inc(wo_zeroed, 1)

            def inverse_deviation(st, pair):
                n = st * (NG // 2) + pair
                cols = bass.ds(pair * (2 * GB), 2 * GB)
                hold(pool, stats_ready, n * 2 + 2, pool_held)
                if not isinstance(n, int) or n > 0:
                    hold(pool, rstd_ready, n, pool_held)
                nc.gpsimd.tensor_tensor(ve[:, :], mv[:, cols, 1:2].rearrange("p b o -> p (b o)"), eps[:, :],
                                        ALU.add).then_inc(ve_ready, 1)
                hold(pool, ve_ready, n + 1, pool_held)
                nc.gpsimd.tensor_tensor(rstd[:, cols], ve[:, :], half[:, :], ALU.pow).then_inc(rstd_ready, 1)

            def add_output_bias(st, g, group):
                hold(pool, xhat_ready, st * NG + g + 1, pool_held)
                rows = xs[:, bass.ds(group * GB, GB), :]
                bias = obias[:, bass.ds(st, 1), :].broadcast_to([128, GB, D])
                nc.gpsimd.tensor_tensor(rows, rows, bias, ALU.add).then_inc(xbias_ready, 1)

            def bias_ahead(st, g, last_pair, nxt):
                if not last_pair:
                    add_output_bias(st, g + 2, g + 2)
                elif nxt is not None:
                    add_output_bias(nxt.stage, g + 2 - NG, g + 2 - NG)

            def normalise(Q, q, keys):
                pool.wait_ge(rinv_ready, Q + 1)
                p = probs[:, q % 2, :, 0:keys]
                r = rinv[:, q % 2, :].unsqueeze(2).broadcast_to([128, 4, keys])
                nc.gpsimd.tensor_tensor(p, p, r, ALU.mult).then_inc(probs_ready, 1)

            def attention(a, nxt, after_attention):
                if a.stage == 1 if a.layer is None else False:
                    zero_wo(FRONT[3], 1)
                if a.stage == 3 if a.layer is None else False:
                    zero_wo(FRONT[5], 2)
                if not after_attention:
                    for q in range(2):
                        normalise(a.number * 64 + q, q, a.keys)

                def group(g, last_pair, last):
                    Q = a.number * 64 + g * QUADS
                    for q in range(1, QUADS + 1):
                        if q + 1 < QUADS or not last or isinstance(nxt, Attention):
                            keys = a.keys if not last or q + 1 < QUADS else nxt.keys
                            normalise(Q + (q + 1), q + 1, keys)
                    bias_ahead(a.stage, g, last_pair, nxt)

                with pool.Fori(0, NG // 2 - 1) as p:
                    group(p * 2, False, False)
                    group(p * 2 + 1, False, False)
                    inverse_deviation(a.stage + 1, p)
                if a.layer is None and a.number in (0, 1):
                    zero_qkv(FRONT[3 if a.number == 0 else 5])
                group(NG - 2, True, False)
                group(NG - 1, True, True)
                inverse_deviation(a.stage + 1, NG // 2 - 1)

            def feed_forward(f, nxt, after_attention):
                with pool.Fori(0, NG // 2 - 1) as p:
                    bias_ahead(f.stage, p * 2, False, nxt)
                    bias_ahead(f.stage, p * 2 + 1, False, nxt)
                    if nxt is not None:
                        inverse_deviation(f.stage + 1, p)
                bias_ahead(f.stage, NG - 2, True, nxt)
                bias_ahead(f.stage, NG - 1, True, nxt)
                if nxt is not None:
                    inverse_deviation(f.stage + 1, NG // 2 - 1)

            for pair in range(NG // 2):
                inverse_deviation(0, pair)
            add_output_bias(0, 0, 0)
            add_output_bias(0, 1, 1)

            def run(stage, nxt, after_attention):
                (attention if isinstance(stage, Attention) else feed_forward)(stage, nxt, after_attention)

            run_network(pool, run)

        @block.scalar
        def _(act):
            def evacuate_q(n, par, c, scale):
                act.wait_ge(q_in_psum, n + 1)
                nc.scalar.activation(qT[:, par, c, :], q_ps[:, 0:GN], ACT.Copy, scale=scale).then_inc(q_ready, 1)

            def evacuate_v(n, par, v, keys):
                act.wait_ge(v_in_psum, n + 1)
                nc.scalar.activation(v_sb[0:keys, par, v // 2, (v % 2) * 512:(v % 2) * 512 + 512],
                                     y_ps[0:keys, :], ACT.Copy).then_inc(v_ready, 1)

            def exponentials(Q, q, keys):
                act.wait_ge(negmax_ready, Q + 1)
                if isinstance(Q, int) and Q < 2:
                    pass
                else:
                    act.wait_ge(pT_in_psum, Q - 1)
                for h in range(4):
                    e = nc.scalar.activation(probs[:, q % 2, h, 0:keys], score_ps[q % 2][:, h, 0:keys], ACT.Exp,
                                             bias=negmax[:, q % 2, h:h + 1], accum_out=sums[:, q % 2, h:h + 1])
                e.then_inc(exp_ready, 1)

            def evacuate_pT(Q, q, keys):
                act.wait_ge(pT_in_psum, Q + 1)
                nc.scalar.activation(pT[0:keys, q % 4, :, :], pT_ps[q % 2][0:keys, :, :], ACT.Copy)\
                    .then_inc(pT_ready, 1)

            def evacuate_group(a, g):
                for c in range(CH):
                    evacuate_q(a.number * 64 + g * CH + c, 0, c, a.scale)
                for v in range(2 * GB):
                    evacuate_v(a.number * 32 + g * 4 + v, 0, v, a.keys)

            def attention(a, nxt, after_attention):
                if after_attention is None:
                    evacuate_group(a, 0)
                if not after_attention:
                    for q in range(2):
                        exponentials(a.number * 64 + q, q, a.keys)
                    evacuate_pT(a.number * 64, 0, a.keys)

                def group(g, par, last):
                    Q = a.number * 64 + g * QUADS
                    b = nxt if last else a
                    for q in range(1, QUADS + 1):
                        if q + 1 < QUADS or isinstance(b, Attention):
                            exponentials(Q + (q + 1), q + 1, a.keys if q + 1 < QUADS else b.keys)
                        if isinstance(b, Attention):
                            cs = QK_AT.get(q, ())
                            for c in cs[:1]:
                                evacuate_q(a.number * 64 + (g + 1) * CH + c, 1 - par, c, b.scale)
                            if q in V_AT:
                                evacuate_v(a.number * 32 + (g + 1) * 4 + V_AT[q], 1 - par, V_AT[q], b.keys)
                            for c in cs[1:]:
                                evacuate_q(a.number * 64 + (g + 1) * CH + c, 1 - par, c, b.scale)
                        if q < QUADS or isinstance(b, Attention):
                            evacuate_pT(Q + q, q, a.keys if q < QUADS else b.keys)

                with act.Fori(0, NG // 2 - 1) as p:
                    group(p * 2, 0, False)
                    group(p * 2 + 1, 1, False)
                group(NG - 2, 0, False)
                group(NG - 1, 1, True)

            def feed_forward(f, nxt, after_attention):
                nc.scalar.activation(hb[:, :], hbias[:, bass.ds(f.number, 1), :].rearrange("p a b -> p (a b)"),
                                     ACT.Copy).then_inc(hb_ready, 1)
                act.wait_ge(hb_ready, f.number + 1)

                def activate(g, par):
                    for c in range(FC):
                        n = f.number * 32 + g * FC + c
                        act.wait_ge(hidden_in_psum, n + 1)
                        b = FC + c if f.gated else c
                        dst = gate[:, c % 2, :] if f.gated else hid[:, par, c, :]
                        nc.scalar.activation(dst, score_ps[c % 2][:, :, :].rearrange("p a b -> p (a b)")[:, 0:GN],
                                             ACT.Gelu, bias=hb[:, b:b + 1])\
                            .then_inc(gate_ready if f.gated else hid_ready, 1)

                with act.Fori(0, NG // 2) as p:
                    activate(p * 2, 0)
                    activate(p * 2 + 1, 1)
                if nxt is not None:
                    evacuate_group(nxt, 0)

            act.wait_ge(params_loaded, 64)

            def run(stage, nxt, after_attention):
                (attention if isinstance(stage, Attention) else feed_forward)(stage, nxt, after_attention)

            run_network(act, run)

        @block.vector
        def _(dve):
            def statistics(b, n, src, keep=None):
                nc.vector.bn_stats(bnst[:, :], src).then_inc(bn_ready, 1)
                if keep is not None:
                    keep()
                hold(dve, bn_ready, n + 1, dve_held)
                nc.vector.bn_aggr(mv_row[:, :], bnst[:, :]).then_inc(aggr_ready, 1)
                hold(dve, aggr_ready, n + 1, dve_held)
                return nc.vector.tensor_copy(mv[:, bass.ds(b, 1), :].rearrange("p a d -> p (a d)"), mv_row[:, :])

            def split_part(a, matrix, half):
                hold(dve, w_loaded, (a.number + 1) * (16 * QKV_DMAS), dve_held)
                n = a.number * W_PARTS + matrix * 2 + half
                cols = slice(half * 512, half * 512 + 512)

                def part(t):
                    return t.rearrange("p a n -> p (a n)")

                raw = part(w_raw[:, bass.ds(matrix, 1), cols])
                hi = part(w_hi[:, a.slot, bass.ds(matrix, 1), cols])
                lo = part(w_lo[:, a.slot, bass.ds(matrix, 1), cols])
                nc.vector.tensor_copy(hi, raw).then_inc(w_hi_ready, 1)
                dve.wait_ge(w_hi_ready, n + 1)
                nc.vector.tensor_tensor(lo, raw, hi, ALU.subtract).then_inc(w_split, 1)

            def split_w1(f):
                wide = (2 if f.gated else 1) * FF
                dve.wait_ge(ff_loaded, (f.number + 1) * (16 * FF_DMAS))
                nc.vector.tensor_copy(w1_hi[:, 0:wide], w1_raw[:, 0:wide]).then_inc(w1_hi_ready, 1)
                dve.wait_ge(w1_hi_ready, f.number + 1)
                nc.vector.tensor_tensor(w1_lo[:, 0:wide], w1_raw[:, 0:wide], w1_hi[:, 0:wide], ALU.subtract)\
                    .then_inc(w1_split, 1)

            def normalise_rows(st, g, pair):
                hold(dve, rstd_ready, st * (NG // 2) + pair + 1, dve_held)
                for i in range(GB):
                    b = g * GB + i
                    op = nc.vector.tensor_scalar(
                        xhat[:, i, :], xs[:, bass.ds(b, 1), :].rearrange("p a d -> p (a d)"),
                        mv[:, bass.ds(b, 1), 0:1].rearrange("p a d -> p (a d)"),
                        rstd[:, bass.ds(b, 1)], ALU.subtract, ALU.mult)
                op.then_inc(xhat_ready, 1)

            def take_hT(st, g, cross=False):
                N = st * NG + g
                dve.wait_ge(hT_in_psum, N + 1)
                gain = norm_sb[:, bass.ds(st, 1), 0:1].rearrange("p a d -> p (a d)")
                shift = norm_sb[:, bass.ds(st, 1), 1:2].rearrange("p a d -> p (a d)")
                nc.vector.tensor_scalar(hT[:, :], k_ps[:, 0:GN], gain, shift, ALU.mult, ALU.add)\
                    .then_inc(hT_affine, 1)
                if cross:
                    src = ctx_sb[:, bass.ds(g * (GB * T), GB * T)]
                    nc.vector.tensor_copy(c_hi[:, :], src)
                dve.wait_ge(hT_affine, N + 1)
                nc.vector.tensor_copy(h_hi[:, :], hT[:, :]).then_inc(h_hi_ready, 1)
                dve.wait_ge(h_hi_ready, N + 1)
                if cross:
                    nc.vector.tensor_tensor(c_lo[:, :], src, c_hi[:, :], ALU.subtract)
                nc.vector.tensor_tensor(h_lo[:, :], hT[:, :], h_hi[:, :], ALU.subtract).then_inc(hT_ready, 1)

            def update_x(st, b, y, with_stats_done, with_stats=True):
                n = st * B + b
                if not with_stats:
                    dve.wait_ge(x_updated, n)
                dve.wait_ge(y_in_psum, n + 1)
                row = xs[:, bass.ds(b, 1), :].rearrange("p a d -> p (a d)")
                nc.vector.tensor_tensor(x_row[:, :], y[:, 0:D], row, ALU.add).then_inc(y_taken, 1)

                def keep():
                    nc.vector.tensor_copy(row, x_row[:, :]).then_inc(x_updated, 1)

                if not with_stats:
                    hold(dve, y_taken, n + 2, dve_held)
                    keep()
                    return
                dve.wait_ge(y_taken, n + 2)
                op = statistics(b, n + B, x_row[:, :], keep)
                if with_stats_done:
                    op.then_inc(stats_ready, 1)

            def row_max(Q, q, keys):
                dve.wait_ge(scores_ready, Q + 1)
                nc.vector.tensor_reduce(negmax[:, q % 2, :], score_ps[q % 2][:, :, 0:keys], AX.X, ALU.max,
                                        negate=True).then_inc(negmax_ready, 1)

            def inverse_sum(Q, q):
                dve.wait_ge(exp_ready, Q + 1)
                nc.vector.reciprocal(rinv[:, q % 2, :], sums[:, q % 2, :]).then_inc(rinv_ready, 1)

            def evacuate_k(n, par, c, keys):
                dve.wait_ge(k_in_psum, n + 1)
                nc.vector.tensor_copy(kT[:, par, c, 0:GB * keys], k_ps[:, 0:GB * keys]).then_inc(k_ready, 1)

            def evacuate_out(n, m):
                dve.wait_ge(av_ready, n + 1)
                nc.vector.tensor_copy(outT[:, m // 2, 4 * (m % 2):4 * (m % 2) + 4, :],
                                      o_ps[:, :].rearrange("p (c s) -> p c s", c=4)).then_inc(outT_ready, 1)

            def gated_product(f, g, par):
                gates_before = 0 if isinstance(f.number, int) and f.number == 0 else 32
                for c in range(FC if f.gated else 0):
                    dve.wait_ge(gate_ready, gates_before + g * FC + c + 1)
                    bias = hbias[:, bass.ds(f.number, 1), c:c + 1].rearrange("p a b -> p (a b)")
                    nc.vector.scalar_tensor_tensor(
                        hid[:, par, c, :], pT_ps[c % 2][:, :, :].rearrange("p a b -> p (a b)")[:, 0:GN],
                        bias, gate[:, c % 2, :], ALU.add, ALU.mult).then_inc(hid_ready, 1)

            def ahead(st, g, last_pair, pair, nxt):
                if not last_pair:
                    return st, g + 2, pair + 1, g + 2
                if nxt is None:
                    return None
                return nxt.stage, g + 2 - NG, 0, g + 2 - NG

            def attention(a, nxt, after_attention):
                following = next_attention(a, nxt)
                if not after_attention:
                    n = a.number * 64
                    row_max(n, 0, a.keys)
                    row_max(n + 1, 1, a.keys)
                    inverse_sum(n, 0)
                    row_max(n + 2, 2, a.keys)
                    inverse_sum(n + 1, 1)

                def group(g, par, pair, last_pair, last, part=None):
                    Q = a.number * 64 + g * QUADS
                    b = nxt if last else a
                    two_ahead = ahead(a.stage, g, last_pair, pair, nxt)
                    crossing = is_cross(nxt) if last_pair else a.cross
                    for q in range(1, QUADS + 1):
                        if q + 2 < QUADS or isinstance(b, Attention):
                            row_max(Q + (q + 2), q + 2, a.keys if q + 2 < QUADS else b.keys)
                        if q % 2 == 0:
                            evacuate_out(a.number * 32 + g * 4 + (q // 2 - 1), q // 2 - 1)
                        if isinstance(b, Attention):
                            for c in QK_AT.get(q, ()):
                                evacuate_k(a.number * 64 + (g + 1) * CH + c, 1 - par, c, b.keys)
                        if q + 1 < QUADS or isinstance(b, Attention):
                            inverse_sum(Q + (q + 1), q + 1)
                        if q == 4 and part is not None and following is not None:
                            split_part(following, part, par)
                        if q == 4 and last_pair and not last and isinstance(nxt, FeedForward):
                            split_w1(nxt)
                        if two_ahead is not None and q == 6:
                            normalise_rows(two_ahead[0], two_ahead[1], two_ahead[2])
                        if q == QUADS and isinstance(b, FeedForward):
                            gated_product(b, 0, 0)
                        if two_ahead is not None and q == QUADS:
                            take_hT(two_ahead[0], two_ahead[1], crossing)
                        if q == OUT_AT[0]:
                            dve.wait_ge(xbias_ready, a.stage * NG + g + 1)
                        if q in OUT_AT:
                            i = OUT_AT.index(q)
                            update_x(a.stage, g * GB + i, y_ps, i == 1)

                with dve.Fori(0, NG // 2 - 1) as p:
                    group(p * 2, 0, p, False, False, p)
                    group(p * 2 + 1, 1, p, False, False, p)
                group(NG - 2, 0, NG // 2 - 1, True, False)
                group(NG - 1, 1, NG // 2 - 1, True, True)

            def feed_forward(f, nxt, after_attention):
                def group(g, par, pair, last_pair, last):
                    two_ahead = ahead(f.stage, g, last_pair, pair, nxt)
                    if two_ahead is not None:
                        normalise_rows(two_ahead[0], two_ahead[1], two_ahead[2])
                    if not last:
                        gated_product(f, g + 1, 1 - par)
                    elif nxt is not None:
                        for c in range(CH):
                            evacuate_k(nxt.number * 64 + c, 0, c, nxt.keys)
                    if two_ahead is not None:
                        take_hT(two_ahead[0], two_ahead[1], last_pair and nxt.cross)
                    dve.wait_ge(xbias_ready, f.stage * NG + g + 1)
                    update_x(f.stage, g * GB, y_ps, False, nxt is not None)
                    update_x(f.stage, g * GB + 1, o_ps, True, nxt is not None)

                with dve.Fori(0, NG // 2 - 1) as p:
                    group(p * 2, 0, p, False, False)
                    group(p * 2 + 1, 1, p, False, False)
                group(NG - 2, 0, NG // 2 - 1, True, False)
                group(NG - 1, 1, NG // 2 - 1, True, True)

            dve.sem_inc(outT_ready, 1)
            dve.sem_inc(y_taken, 1)
            dve.wait_ge(x_loaded, 16)
            for b in range(B):
                op = statistics(b, b, xs[:, b, :])
                if b % GB == GB - 1:
                    op.then_inc(stats_ready, 1)
            dve.wait_ge(params_loaded, 64)
            first = FRONT[0]
            for part in range(W_PARTS):
                split_part(first, part // 2, part % 2)
            normalise_rows(0, 0, 0)
            take_hT(0, 0)
            normalise_rows(0, 1, 0)
            for c in range(CH):
                evacuate_k(c, 0, c, first.keys)
            take_hT(0, 1)

            def run(stage, nxt, after_attention):
                (attention if isinstance(stage, Attention) else feed_forward)(stage, nxt, after_attention)

            run_network(dve, run)

        @block.tensor
        def _(pe):
            pe.wait_ge(ident_ready, 1)

            def project_group(a, g):
                for c in range(CH):
                    project_qk(a, a.number * 64 + g * CH + c, c, a.number * 32 + g * 4)
                for v in range(2 * GB):
                    project_v(a, a.number * 32 + g * 4 + v, v, 0)

            def transpose_rows(st, g, k_before):
                N = st * NG + g
                pe.wait_ge(xhat_ready, N + 1)
                at_least(pe, k_ready, k_before)
                at_least(pe, hT_ready, N)
                for i in range(GB):
                    m = nc.tensor.transpose(k_ps[:, i * S:(i + 1) * S], xhat[:, i, :], ident[:, :])
                m.then_inc(hT_in_psum, 1)

            def three_passes(dst, l_hi, l_lo, r_hi, r_lo):
                nc.tensor.matmul(dst, l_hi, r_lo, start=True, stop=False)
                nc.tensor.matmul(dst, l_lo, r_hi, start=False, stop=False)
                return nc.tensor.matmul(dst, l_hi, r_hi, start=False, stop=True)

            def project_qk(a, n, c, v_before):
                cols = slice(c * 128, c * 128 + 128)
                at_least(pe, q_ready, n)
                three_passes(q_ps[:, 0:GN], w_hi[:, a.slot, 0, cols], w_lo[:, a.slot, 0, cols], h_hi[:, :],
                             h_lo[:, :]).then_inc(q_in_psum, 1)
                at_least(pe, k_ready, n)
                s_hi, s_lo = (c_hi, c_lo) if a.cross else (h_hi, h_lo)
                three_passes(k_ps[:, 0:GB * a.keys], w_hi[0:a.rows, a.slot, 1, cols], w_lo[0:a.rows, a.slot, 1, cols],
                             s_hi[:, :], s_lo[:, :]).then_inc(k_in_psum, 1)

            def project_v(a, n, v, y_before):
                s_hi, s_lo = (c_hi, c_lo) if a.cross else (h_hi, h_lo)
                i, cols = v // 2, slice((v % 2) * 512, (v % 2) * 512 + 512)
                rows = slice(i * a.keys, (i + 1) * a.keys)
                at_least(pe, v_ready, n)
                if not (isinstance(y_before, int) and y_before == 0):
                    pe.wait_ge(y_taken, y_before + 1)
                three_passes(y_ps[0:a.keys, :], s_hi[:, rows], s_lo[:, rows],
                             w_hi[0:a.rows, a.slot, 2, cols], w_lo[0:a.rows, a.slot, 2, cols])\
                    .then_inc(v_in_psum, 1)

            def scores(Q, q, par, keys):
                if not isinstance(Q, int) or Q >= 2:
                    pe.wait_ge(exp_ready, Q - 1)
                i, j = (q // 4) % GB, q % 4
                lo = SLOT * (q % 2)
                for h in range(4):
                    c = 4 * (j // 2) + h
                    m = nc.tensor.matmul(score_ps[q % 2][:, h, 0:keys],
                                         qT[lo:lo + SLOT, par, c, i * S:(i + 1) * S],
                                         kT[lo:lo + SLOT, par, c, i * keys:(i + 1) * keys], start=True, stop=True)
                m.then_inc(scores_ready, 1)

            def transpose_probs(Q, q, keys):
                pe.wait_ge(probs_ready, Q + 1)
                for h in range(4):
                    m = nc.tensor.transpose(pT_ps[q % 2][0:keys, h, :], probs[:, q % 2, h, 0:keys], ident[:, :])
                m.then_inc(pT_in_psum, 1)

            def weigh_values(Q, n, q, par, keys):
                pe.wait_ge(pT_ready, Q + 2)
                pe.wait_ge(outT_ready, n + 1)
                for h in range(4):
                    for odd in range(2):
                        head = 2 * (4 * ((q % 4) // 2) + h) + odd
                        m = nc.tensor.matmul(o_ps[odd * SLOT:(odd + 1) * SLOT, h * S:(h + 1) * S],
                                             v_sb[0:keys, par, q // 4, head * SLOT:(head + 1) * SLOT],
                                             pT[0:keys, (q + odd) % 4, h, :], start=True, stop=True)
                m.then_inc(av_ready, 1)

            def project_out(a, b, pairs_done, slot, v_before):
                pe.wait_ge(wo_loaded[a.slot], (a.turn + 1) * (16 * WO_DMAS))
                pe.wait_ge(outT_ready, pairs_done + 1)
                pe.wait_ge(y_taken, a.stage * B + b + 1)
                at_least(pe, v_ready, v_before)
                for c in range(CH):
                    m = nc.tensor.matmul(y_ps[:, 0:D], outT[:, slot, c, :], wo_sb[:, a.slot, c, :],
                                         start=(c == 0), stop=(c == CH - 1))
                m.then_inc(y_in_psum, 1)

            def attention(a, nxt, after_attention):
                k0, v0 = a.number * 64, a.number * 32
                if not after_attention:
                    pe.wait_ge(q_ready, k0 + CH)
                    pe.wait_ge(k_ready, k0 + CH)
                    for q in range(3):
                        scores(a.number * 64 + q, q, 0, a.keys)
                    transpose_probs(a.number * 64, 0, a.keys)
                def group(g, par, last_pair, last):
                    Q = a.number * 64 + g * QUADS
                    n = a.number * 32 + g * 4
                    b = nxt if last else a
                    on = isinstance(b, Attention)
                    v_after = v0 + (g + 1) * 4
                    for q in range(1, QUADS + 1):
                        if q == 1:
                            pe.wait_ge(v_ready, v0 + g * 4 + 4)
                            if on:
                                pe.wait_ge(hT_ready, a.stage * NG + g + 2)
                                if last:
                                    pe.wait_ge(w_split, (nxt.number + 1) * W_PARTS)
                        if q in (QUADS - 2, QUADS) and on:
                            pe.wait_ge(q_ready, k0 + (g + 1) * CH + (4 if q < QUADS else CH))
                            pe.wait_ge(k_ready, k0 + (g + 1) * CH + (4 if q < QUADS else CH))
                        if q + 2 < QUADS:
                            scores(Q + (q + 2), q + 2, par, a.keys)
                        elif on:
                            scores(Q + (q + 2), q + 2, 1 - par, b.keys)
                        cs = QK_AT.get(q, ()) if on else ()
                        v_done = sum(1 for s in V_AT if s < q)
                        y_before = a.stage * B + g * GB + (0 if q <= OUT_AT[0] else 1)
                        for c in cs[:1]:
                            project_qk(b, k0 + (g + 1) * CH + c, c, None)
                        if q % 2 == 0:
                            weigh_values(Q + (q - 2), n + (q // 2 - 1), q - 2, par, a.keys)
                        if on and q in V_AT:
                            project_v(b, v_after + V_AT[q], V_AT[q], y_before)
                        for c in cs[1:]:
                            project_qk(b, k0 + (g + 1) * CH + c, c, None)
                        if q == QUADS:
                            if isinstance(b, FeedForward):
                                start_hidden(b)
                            if not last_pair:
                                transpose_rows(a.stage, g + 2, k0 + (g + 2) * CH)
                            elif nxt is not None:
                                transpose_rows(nxt.stage, g + 2 - NG,
                                               k0 + (g + 1) * CH + (CH if on else 0))
                        if q < QUADS:
                            transpose_probs(Q + q, q, a.keys)
                        elif on:
                            transpose_probs(Q + q, q, b.keys)
                        if q in OUT_AT:
                            i = OUT_AT.index(q)
                            v_by_now = v_after + (sum(1 for s in V_AT if s <= q) if on else 0)
                            project_out(a, g * GB + i, n + 2 * (i + 1), i, v_by_now)

                with pe.Fori(0, NG // 2 - 1) as p:
                    group(p * 2, 0, False, False)
                    group(p * 2 + 1, 1, False, False)
                group(NG - 2, 0, True, False)
                group(NG - 1, 1, True, True)

            def flat(bank):
                return bank[:, :, :].rearrange("p a b -> p (a b)")[:, 0:GN]

            def hidden(f, g):
                pe.wait_ge(hT_ready, f.stage * NG + g + 1)
                for c in range(FC):
                    n = f.number * 32 + g * FC + c
                    if not isinstance(n, int) or n >= 2:
                        pe.wait_ge(hid_ready, n - 1)
                    if f.gated:
                        cols = slice(c * 128, c * 128 + 128)
                        three_passes(flat(pT_ps[c % 2]), w1_hi[:, cols], w1_lo[:, cols], h_hi[:, :], h_lo[:, :])
                    b = FC + c if f.gated else c
                    cols = slice(b * 128, b * 128 + 128)
                    three_passes(flat(score_ps[c % 2]), w1_hi[:, cols], w1_lo[:, cols], h_hi[:, :], h_lo[:, :])\
                        .then_inc(hidden_in_psum, 1)

            def start_hidden(f):
                pe.wait_ge(w1_split, f.number + 1)
                pe.wait_ge(exp_ready, f.attentions * 64)
                pe.wait_ge(pT_ready, f.attentions * 64)
                hidden(f, 0)

            def feed_forward(f, nxt, after_attention):
                k0, v0 = f.attentions * 64, f.attentions * 32

                def second(g, par):
                    pe.wait_ge(ff_loaded, (f.number + 1) * (16 * FF_DMAS))
                    pe.wait_ge(hid_ready, f.number * 32 + g * FC + FC)
                    for i, y in enumerate((y_ps, o_ps)):
                        pe.wait_ge(y_taken, f.stage * B + g * GB + 1)
                        for c in range(FC):
                            m = nc.tensor.matmul(y[:, 0:D], hid[:, par, c, i * S:(i + 1) * S], w2_sb[:, c, :],
                                                 start=(c == 0), stop=(c == FC - 1))
                        m.then_inc(y_in_psum, 1)

                def group(g, par, last_pair, last):
                    if not last:
                        hidden(f, g + 1)
                    elif nxt is not None:
                        pe.wait_ge(hT_ready, nxt.stage * NG + 1)
                        pe.wait_ge(w_split, (nxt.number + 1) * W_PARTS)
                        pe.wait_ge(y_taken, f.stage * B + g * GB + 1)
                        project_group(nxt, 0)
                        pe.wait_ge(v_ready, v0 + 4)
                    if not last_pair:
                        transpose_rows(f.stage, g + 2, k0)
                    elif nxt is not None:
                        transpose_rows(nxt.stage, g + 2 - NG, k0 + (CH if last else 0))
                    second(g, par)

                with pe.Fori(0, NG // 2 - 1) as p:
                    group(p * 2, 0, False, False)
                    group(p * 2 + 1, 1, False, False)
                group(NG - 2, 0, True, False)
                group(NG - 1, 1, True, True)

            first = FRONT[0]
            transpose_rows(0, 0, 0)
            pe.wait_ge(hT_ready, 1)
            pe.wait_ge(w_split, W_PARTS)
            project_group(first, 0)
            transpose_rows(0, 1, CH)

            def run(stage, nxt, after_attention):
                (attention if isinstance(stage, Attention) else feed_forward)(stage, nxt, after_attention)

            run_network(pe, run)


def kernel(**inputs):
    import numpy as np
    from concourse.bacc import Bacc
    from concourse.bass_utils import run_bass_kernel_spmd

    nc = Bacc("TRN2", target_bir_lowering=False, num_devices=1)
    arrays = {}

    def dram(name, a):
        a = np.ascontiguousarray(a)
        arrays[name] = a
        return nc.dram_tensor(name, a.shape, mybir.dt.from_np(a.dtype), kind="ExternalInput").ap()

    def given(name):
        return dram(name, inputs[name])

    L0, L1, L2, L3 = (f"L{i}_xattn_" for i in range(4))
    pairs = [(L0 + "ln1_g", L0 + "ln1_b"), (L0 + "ln2_g", L0 + "ln2_b"), (L0 + "ln3_g", L0 + "ln3_b"),
             (L1 + "n1_g", L1 + "n1_b"), (L1 + "n2_g", L1 + "n2_b"), (L1 + "n3_g", L1 + "n3_b"),
             (L1 + "n4_g", L1 + "n4_b"),
             (L2 + "g1", L2 + "be1"), (L2 + "g2", L2 + "be2"), (L2 + "g3", L2 + "be3")]
    biases = [L0 + "sa_bo", L0 + "ca_bo", L0 + "ff_b2", L1 + "so_b", L1 + "f1_b2", L1 + "co_b", L1 + "f2_b2",
              L2 + "bo1", L2 + "bo2", L2 + "b2"]
    gains = [np.asarray(inputs[g]) for g, _ in pairs]
    shifts = [np.asarray(inputs[b]) for _, b in pairs]
    rows = [np.asarray(inputs[b]) for b in biases]
    for i in range(DEPTH3):
        for n, b in (("ln1", "b_sa_o"), ("ln2", "b_ca_o"), ("ln3", "b_ff2")):
            gains.append(np.asarray(inputs[f"{L3}{n}_g"])[i])
            shifts.append(np.asarray(inputs[f"{L3}{n}_b"])[i])
            rows.append(np.asarray(inputs[L3 + b])[i])
    norms = dram("norms", np.stack([np.stack(gains, 1), np.stack(shifts, 1)], 2))
    out_biases = dram("out_biases", np.stack(rows))
    hidden = []
    for b in (inputs[L0 + "ff_b1"], inputs[L1 + "f1_b1"], inputs[L1 + "f2_b1"], inputs[L2 + "bp"],
              *np.asarray(inputs[L3 + "b_ff1"])):
        h = np.zeros((128, 2 * FC), np.float32)
        h[:, :len(b) // 128] = np.asarray(b).reshape(-1, 128).T
        hidden.append(h)
    hidden_biases = dram("hidden_biases", np.stack(hidden, 1))
    ctxT = dram("ctxT", np.asarray(inputs["ctx_768"]).transpose(2, 0, 1).reshape(C, B * T))

    attn_w = {
        0: [given(L0 + n) for n in ("sa_wq", "sa_wk", "sa_wv", "sa_wo")],
        1: [given(L0 + n) for n in ("ca_wq", "ca_wk", "ca_wv", "ca_wo")],
        4: [given(L2 + n) for n in ("Wq1", "Wk1", "Wv1", "Wo1")],
        5: [given(L2 + n) for n in ("Wq2", "Wk2", "Wv2", "Wo2")],
    }
    thin_w = {"self": [given(L1 + n) for n in ("sq_w", "sk_w", "sv_w", "so_w")],
              "cross": [given(L1 + n) for n in ("cq_w", "ck_w", "cv_w", "co_w")]}
    ff_w = {0: (given(L0 + "ff_w1"), given(L0 + "ff_w2")), 1: (given(L1 + "f1_w1"), given(L1 + "f1_w2")),
            2: (given(L1 + "f2_w1"), given(L1 + "f2_w2")), 3: (given(L2 + "Wp"), given(L2 + "W2"))}
    qkv, sao, wq, kv, cao, ff1, ff2 = (given(L3 + n) for n in
                                       ("w_qkv", "w_sa_o", "w_q", "w_kv", "w_ca_o", "w_ff1", "w_ff2"))

    def of_layer(w, lo=None, hi=None):
        cols = slice(0, w.shape[2]) if lo is None else slice(lo, hi)
        return lambda layer: w[bass.ds(layer, 1), :, cols].rearrange("a p n -> (a p) n")

    deep_w = {
        "self": [of_layer(qkv, 0, INNER), of_layer(qkv, INNER, 2 * INNER), of_layer(qkv, 2 * INNER, 3 * INNER),
                 of_layer(sao)],
        "cross": [of_layer(wq), of_layer(kv, 0, INNER), of_layer(kv, INNER, 2 * INNER), of_layer(cao)],
        "ff": [of_layer(ff1), of_layer(ff2)],
    }
    out = nc.dram_tensor("out", (B, S, D), F32, kind="ExternalOutput").ap()
    build(nc, given("x"), ctxT, norms, out_biases, hidden_biases, attn_w, thin_w, ff_w, deep_w, out)
    r = run_bass_kernel_spmd(nc, [arrays], core_ids=[0])
    return r.results[0]["out"]
```

```python
from contextlib import ExitStack

import concourse.bass as bass
from concourse import mybir

F32 = mybir.dt.float32
F32R = mybir.dt.float32r
ALU = mybir.AluOpType
ACT = mybir.ActivationFunctionType
AX = mybir.AxisListType

B, S, D = 16, 128, 128
T, C = 120, 96
HEADS, SLOT = 16, 64
INNER = HEADS * SLOT
THIN = 8
FF = 4 * D
EPS = 1e-5

GB = 2
NG = B // GB
GN = GB * S
QUADS = GB * 4
CH = INNER // 128
FC = FF // 128
DEPTH3 = 4
STAGES, ATTNS, FFS = 10 + 3 * DEPTH3, 6 + 2 * DEPTH3, 4 + DEPTH3

PE_PLAN = {1: "s q0 k0 v0 q1 t k1", 2: "s q2 k2 a t", 3: "q3 s v1 k3 t", 4: "s q4 k4 a v2 q5 k5 t",
           5: "s k6 q6 o t", 6: "s q7 k7 a t", 7: "v3 s t", 8: "s a h t o"}
ACT_PLAN = {1: "e q0 v0 q1 p", 2: "e q2 p", 3: "e q3 v1 p", 4: "e q4 v2 q5 p",
            5: "q6 e p", 6: "q7 e p", 7: "e p v3", 8: "e p"}
DVE_PLAN = {1: "k0 r m k1", 2: "m k2 x r", 3: "m r k3", 4: "m k4 x k5 r w",
            5: "m r k6 u", 6: "m k7 x r n", 7: "r m", 8: "m x r h u"}
PE_THIN = {1: "q0 s k0 v0 q1 k1 t", 2: "s q2 k2 a t", 3: "q3 s k3 t", 4: "s a v2 t", 5: "s o t",
           6: "s a t", 7: "s t", 8: "s a h t o"}
ACT_THIN = {1: "e q0 v0 q1 p", 2: "q2 e p", 3: "e q3 p", 4: "e v2 p", 5: "e p",
           6: "e p", 7: "e p", 8: "e p"}
DVE_THIN = {1: "k0 r m k1", 2: "m k2 x r", 3: "m r k3", 4: "m x r w", 5: "m r u",
           6: "m x r n", 7: "r m", 8: "m x r h u"}
QKV_DMAS, WO_DMAS, FF_DMAS = 3, 2, 2
W_PARTS = 6


class Attention:

    def __init__(self, stage, number, cross=False, thin=False, layer=None):
        self.stage, self.number, self.cross, self.thin, self.layer = stage, number, cross, thin, layer
        self.keys, self.rows = (T, C) if cross else (S, D)
        self.slot = int(cross)
        self.turn = number // 2 if isinstance(number, int) else layer + 3
        self.scale = float(THIN if thin else SLOT) ** -0.5
        self.space = SLOT // 2 if thin else SLOT
        self.chunks = HEADS * self.space // 128
        self.counts = CH // self.chunks

    def head_of(self, quad, h):
        j = quad % 4
        return (h, self.space * j) if self.thin else (4 * (j // 2) + h, self.space * (j % 2))


class FeedForward:

    def __init__(self, stage, number, gated=False, layer=None, before=None):
        self.stage, self.number, self.gated, self.layer = stage, number, gated, layer
        self.attentions = before


def deep_layer(layer):
    return [Attention(layer * 3 + 10, layer * 2 + 6, layer=layer),
            Attention(layer * 3 + 11, layer * 2 + 7, cross=True, layer=layer),
            FeedForward(layer * 3 + 12, layer + 4, layer=layer, before=layer * 2 + 8)]


FRONT = [Attention(0, 0), Attention(1, 1, cross=True), FeedForward(2, 0, gated=True, before=2),
         Attention(3, 2, thin=True), FeedForward(4, 1, before=3), Attention(5, 3, cross=True, thin=True),
         FeedForward(6, 2, before=4),
         Attention(7, 4), Attention(8, 5, cross=True), FeedForward(9, 3, gated=True, before=6)]


def run_network(eng, run):
    def run_list(stages, following):
        for stage, nxt in zip(stages, stages[1:] + [following]):
            run(stage, nxt)

    run_list(FRONT, deep_layer(0)[0])
    with eng.Fori(0, DEPTH3 - 1) as layer:
        run_list(deep_layer(layer), deep_layer(layer + 1)[0])
    run_list(deep_layer(DEPTH3 - 1), None)


def gates_before(f):
    return 0 if f is FRONT[2] else NG * FC


def items(plan, q):
    return [(w[0], int(w[1:] or 0)) for w in plan[q].split()]


def is_cross(stage):
    return isinstance(stage, Attention) and stage.cross


def next_attention(a, nxt):
    if isinstance(nxt, Attention):
        return nxt
    if a.layer is not None:
        return None if isinstance(a.layer, int) else Attention(a.stage + 2, a.number + 1, layer=a.layer + 1)
    later = [s for s in FRONT if isinstance(s, Attention) and s.number == a.number + 1]
    return later[0] if later else deep_layer(0)[0]


def at_least(eng, sem, value):
    if isinstance(value, int) and value <= 0:
        return
    eng.wait_ge(sem, value)


def hold(eng, sem, value, held):
    eng.wait_ge(sem, value)
    eng.sem_inc(held, 1)


def build(nc, x, ctxT, norms, out_biases, hidden_biases, attn_w, thin_w, ff_w, deep_w, out):
    with ExitStack() as ctx:
        def sb(name, shape, dt=F32):
            return ctx.enter_context(nc.sbuf_tensor(name, shape, dt))

        def psum(name, shape):
            return ctx.enter_context(nc.psum_tensor(name, shape, F32))

        def sem(name):
            return ctx.enter_context(nc.semaphore(name))

        xs = sb("xs", [128, B, D])
        ctx_sb = sb("ctx_sb", [C, B * T])
        norm_sb = sb("norm_sb", [128, STAGES, 2])
        obias = sb("obias", [128, STAGES, D])
        hbias = sb("hbias", [128, FFS, 2 * FC])
        ident = sb("ident", [128, 128])
        eps = sb("eps", [128, 2 * GB])
        half = sb("half", [128, 2 * GB])
        bnst = sb("bnst", [128, GB, 6])
        mv_rows = sb("mv_rows", [128, GB, 2])
        x_rows = sb("x_rows", [128, GB, D])
        mv = sb("mv", [128, B, 2])
        ve = sb("ve", [128, 2 * GB])
        rstd = sb("rstd", [128, B])
        xhat = sb("xhat", [128, GB, D])
        hT = sb("hT", [128, GN])
        h_hi = sb("h_hi", [128, GN], F32R)
        h_lo = sb("h_lo", [128, GN], F32R)
        c_hi = sb("c_hi", [C, GB * T], F32R)
        c_lo = sb("c_lo", [C, GB * T], F32R)
        w_raw = sb("w_raw", [128, 3, INNER])
        w_hi = sb("w_hi", [128, 2, 3, INNER], F32R)
        w_lo = sb("w_lo", [128, 2, 3, INNER], F32R)
        wo_sb = sb("wo_sb", [128, 2, CH, D])
        w1_raw = sb("w1_raw", [128, 2 * FF])
        w1_hi = sb("w1_hi", [128, 2 * FF], F32R)
        w1_lo = sb("w1_lo", [128, 2 * FF], F32R)
        w2_sb = sb("w2_sb", [128, FC, D])
        qT = sb("qT", [128, 2, CH, GN])
        kT = sb("kT", [128, 2, CH, GN])
        v_sb = sb("v_sb", [128, 2, GB, INNER])
        negmax = sb("negmax", [128, 2, 4])
        sums = sb("sums", [128, 2, 4])
        rinv = sb("rinv", [128, 2, 4])
        probs = sb("probs", [128, 2, 4, S])
        pT = sb("pT", [128, 4, 4, S])
        outT = sb("outT", [128, 2, CH, S])
        hb = sb("hb", [128, 2 * FC])
        gate = sb("gate", [128, 2, GN])
        linear = sb("linear", [128, 2, GN])
        hid = sb("hid", [128, 2, FC, GN])

        def flat(bank):
            return bank[:, :] if bank in (q_ps, k_ps) else bank[:, :, :].rearrange("p a b -> p (a b)")

        score_ps = [psum(f"score_ps{i}", [128, 4, 128]) for i in range(2)]
        pT_ps = [psum(f"pT_ps{i}", [128, 4, 128]) for i in range(2)]
        o_ps = psum("o_ps", [128, 512])
        y_ps = psum("y_ps", [128, 512])
        q_ps = psum("q_ps", [128, 512])
        k_ps = psum("k_ps", [128, 512])

        first_loaded = sem("first_loaded")
        x_loaded = sem("x_loaded")
        params_loaded = sem("params_loaded")
        w_loaded = sem("w_loaded")
        wo_loaded = [sem(f"wo{i}_loaded") for i in range(2)]
        wo_zeroed = sem("wo_zeroed")
        ff_loaded = sem("ff_loaded")
        pad_zeroed = sem("pad_zeroed")
        ident_zeroed = sem("ident_zeroed")
        ident_ready = sem("ident_ready")
        constants_ready = sem("constants_ready")
        w_hi_ready = sem("w_hi_ready")
        w_split = sem("w_split")
        w1_hi_ready = sem("w1_hi_ready")
        w1_split = sem("w1_split")
        bn_ready = sem("bn_ready")
        aggr_ready = sem("aggr_ready")
        y_taken = sem("y_taken")
        hb_ready = sem("hb_ready")
        stats_ready = sem("stats_ready")
        ve_ready = sem("ve_ready")
        rstd_ready = sem("rstd_ready")
        xhat_ready = sem("xhat_ready")
        xbias_ready = sem("xbias_ready")
        hT_in_psum = sem("hT_in_psum")
        hT_affine = sem("hT_affine")
        h_hi_ready = sem("h_hi_ready")
        hT_ready = sem("hT_ready")
        q_in_psum = sem("q_in_psum")
        k_in_psum = sem("k_in_psum")
        v_in_psum = sem("v_in_psum")
        q_ready = sem("q_ready")
        k_ready = sem("k_ready")
        v_ready = sem("v_ready")
        scores_ready = sem("scores_ready")
        negmax_ready = sem("negmax_ready")
        exp_ready = sem("exp_ready")
        rinv_ready = sem("rinv_ready")
        probs_ready = sem("probs_ready")
        pT_in_psum = sem("pT_in_psum")
        pT_ready = sem("pT_ready")
        av_ready = sem("av_ready")
        outT_ready = sem("outT_ready")
        y_in_psum = sem("y_in_psum")
        x_updated = sem("x_updated")
        hidden_in_psum = sem("hidden_in_psum")
        gate_ready = sem("gate_ready")
        hid_ready = sem("hid_ready")
        pool_held = sem("pool_held")
        dve_held = sem("dve_held")
        stored = sem("stored")

        block = ctx.enter_context(nc.Block())

        @block.sync
        def _(sp):
            tokens_first = x.rearrange("b s d -> s b d")
            sp.dma_start(xs[:, 0:2 * GB, :], tokens_first[:, 0:2 * GB, :]).then_inc(first_loaded, 16)
            sp.dma_start(norm_sb[:, :, :], norms).then_inc(first_loaded, 16)

            def load_attention(a):
                at_least(sp, w_split, a.number * W_PARTS)
                if a.thin:
                    sp.wait_ge(pad_zeroed, 1 + a.slot)
                if a.layer is not None:
                    q, k, v, wo = [f(a.layer) for f in deep_w["cross" if a.cross else "self"]]
                elif a.thin:
                    q, k, v, wo = thin_w["cross" if a.cross else "self"]
                else:
                    q, k, v, wo = attn_w[a.number]
                width, space = THIN if a.thin else SLOT, a.space
                for n, (w, rows) in enumerate(((q, D), (k, a.rows), (v, a.rows))):
                    dst = w_raw[0:rows, n, 0:HEADS * space].rearrange("p (h e) -> p h e", e=space)[:, :, 0:width]
                    sp.dma_start(dst, w.rearrange("p (h e) -> p h e", e=width)).then_inc(w_loaded, 16)
                return wo, width

            def load_wo(a, wo, width, stages_done):
                at_least(sp, x_updated, stages_done * B)
                if a.thin:
                    sp.wait_ge(wo_zeroed, 1 + a.slot)
                per = 128 // a.space
                parts = wo.rearrange("(c per e) n -> per e c n", per=per, e=width)
                for part in range(per):
                    sp.dma_start(wo_sb[part * a.space:part * a.space + width, a.slot, 0:a.chunks, :],
                                 parts[part]).then_inc(wo_loaded[a.slot], 16)

            def load_ff(f, stages_done):
                at_least(sp, x_updated, stages_done * B)
                w1, w2 = [w(f.layer) for w in deep_w["ff"]] if f.layer is not None else ff_w[f.number]
                sp.dma_start(w1_raw[:, 0:(2 if f.gated else 1) * FF], w1).then_inc(ff_loaded, 16)
                sp.dma_start(w2_sb[:, :, :], w2.rearrange("(c p) n -> p c n", p=128)).then_inc(ff_loaded, 16)

            def load(stage, nxt):
                if isinstance(stage, Attention):
                    wo, width = load_attention(stage)
                    if stage is FRONT[0]:
                        load_rest()
                    load_wo(stage, wo, width, wo_free_after(stage))
                else:
                    load_ff(stage, ff_free_after(stage))

            def wo_free_after(a):
                if a.layer is not None:
                    return a.stage - 2
                return {0: 0, 1: 0, 2: 1, 3: 2, 4: 4, 5: 6}[a.number]

            def ff_free_after(f):
                if f.layer is not None:
                    return f.stage - 2
                return {0: 0, 1: 3, 2: 5, 3: 7}[f.number]

            def load_rest():
                sp.dma_start(xs[:, 2 * GB:B, :], tokens_first[:, 2 * GB:B, :]).then_inc(x_loaded, 16)
                sp.dma_start(hbias[:, :, :], hidden_biases).then_inc(params_loaded, 16)
                sp.dma_start(ctx_sb[:, :], ctxT).then_inc(params_loaded, 16)
                sp.dma_start(obias[:, :, :], out_biases.partition_broadcast(128)).then_inc(params_loaded, 16)

            run_network(sp, load)
            sp.wait_ge(x_updated, B * STAGES)
            sp.dma_start(out.rearrange("b s d -> s b d"), xs[:, :, :]).then_inc(stored, 16)
            sp.wait_ge(stored, 16)

        @block.gpsimd
        def _(pool):
            nc.gpsimd.memset(eps[:, :], EPS).then_inc(constants_ready, 1)
            nc.gpsimd.memset(half[:, :], -0.5).then_inc(constants_ready, 1)
            nc.gpsimd.memset(ident[:, :], 0.0).then_inc(ident_zeroed, 1)
            pool.wait_ge(ident_zeroed, 1)
            nc.gpsimd.affine_select(out=ident[:, :], in_=ident[:, :], compare_op=ALU.not_equal, fill=1.0,
                                    base=0, pattern=[[-1, 128]], channel_multiplier=1).then_inc(ident_ready, 1)
            pool.wait_ge(constants_ready, 2)

            def zero_qkv(a):
                pool.wait_ge(w_split, a.number * W_PARTS)
                nc.gpsimd.memset(w_raw[:, :, :], 0.0).then_inc(pad_zeroed, 1)

            def zero_wo(a, stages_done):
                pool.wait_ge(x_updated, stages_done * B)
                nc.gpsimd.memset(wo_sb[:, a.slot, :, :], 0.0).then_inc(wo_zeroed, 1)

            def inverse_deviation(st, pair):
                n = st * (NG // 2) + pair
                cols = bass.ds(pair * (2 * GB), 2 * GB)
                hold(pool, stats_ready, n * 2 + 2, pool_held)
                if not isinstance(n, int) or n > 0:
                    hold(pool, rstd_ready, n, pool_held)
                nc.gpsimd.tensor_tensor(ve[:, :], mv[:, cols, 1:2].rearrange("p b o -> p (b o)"), eps[:, :],
                                        ALU.add).then_inc(ve_ready, 1)
                hold(pool, ve_ready, n + 1, pool_held)
                nc.gpsimd.tensor_tensor(rstd[:, cols], ve[:, :], half[:, :], ALU.pow).then_inc(rstd_ready, 1)

            def add_output_bias(st, g, group):
                hold(pool, xhat_ready, st * NG + g + 1, pool_held)
                rows = xs[:, bass.ds(group * GB, GB), :]
                bias = obias[:, bass.ds(st, 1), :].broadcast_to([128, GB, D])
                nc.gpsimd.tensor_tensor(rows, rows, bias, ALU.add).then_inc(xbias_ready, 1)

            def bias_ahead(st, g, last_pair, nxt):
                if not last_pair:
                    add_output_bias(st, g + 2, g + 2)
                elif nxt is not None:
                    add_output_bias(nxt.stage, g + 2 - NG, g + 2 - NG)

            def normalise(Q, q, keys):
                pool.wait_ge(rinv_ready, Q + 1)
                p = probs[:, q % 2, :, 0:keys]
                r = rinv[:, q % 2, :].unsqueeze(2).broadcast_to([128, 4, keys])
                nc.gpsimd.tensor_tensor(p, p, r, ALU.mult).then_inc(probs_ready, 1)

            def gated_products(f, g, par):
                for c in range(FC if f.gated else 0):
                    pool.wait_ge(gate_ready, gates_before(f) + g * FC + c + 1)
                    nc.gpsimd.tensor_tensor(hid[:, par, c, :], linear[:, c % 2, :], gate[:, c % 2, :], ALU.mult)\
                        .then_inc(hid_ready, 1)

            def normalise_first(a):
                for q in range(2):
                    normalise(a.number * 64 + q, q, a.keys)

            def attention(a, nxt):
                if a is FRONT[1]:
                    zero_wo(FRONT[3], 1)
                if a is FRONT[3]:
                    zero_wo(FRONT[5], 2)
                def group(g, last_pair, last):
                    Q = a.number * 64 + g * QUADS
                    for q in range(1, QUADS + 1):
                        if q + 1 < QUADS or not last or isinstance(nxt, Attention):
                            keys = a.keys if not last or q + 1 < QUADS else nxt.keys
                            normalise(Q + (q + 1), q + 1, keys)
                    bias_ahead(a.stage, g, last_pair, nxt)

                with pool.Fori(0, NG // 2 - 1) as p:
                    group(p * 2, False, False)
                    group(p * 2 + 1, False, False)
                    inverse_deviation(a.stage + 1, p)
                if a.layer is None and a.number in (0, 1):
                    zero_qkv(FRONT[3 if a.number == 0 else 5])
                group(NG - 2, True, False)
                group(NG - 1, True, True)
                if isinstance(nxt, FeedForward):
                    gated_products(nxt, 0, 0)
                inverse_deviation(a.stage + 1, NG // 2 - 1)

            def feed_forward(f, nxt):
                def group(g, par, last_pair):
                    if not (isinstance(g, int) and g == NG - 1):
                        gated_products(f, g + 1, 1 - par)
                    bias_ahead(f.stage, g, last_pair, nxt)

                group(0, 0, False)
                with pool.Fori(0, NG // 2 - 2) as p:
                    group(p * 2 + 1, 1, False)
                    group(p * 2 + 2, 0, False)
                    if nxt is not None:
                        inverse_deviation(f.stage + 1, p)
                group(NG - 3, 1, False)
                group(NG - 2, 0, True)
                if nxt is not None:
                    inverse_deviation(f.stage + 1, NG // 2 - 2)
                group(NG - 1, 1, True)
                if nxt is not None:
                    normalise_first(nxt)
                    inverse_deviation(f.stage + 1, NG // 2 - 1)

            inverse_deviation(0, 0)
            pool.wait_ge(params_loaded, 48)
            add_output_bias(0, 0, 0)
            add_output_bias(0, 1, 1)
            normalise_first(FRONT[0])
            for pair in range(1, NG // 2):
                inverse_deviation(0, pair)

            def run(stage, nxt):
                (attention if isinstance(stage, Attention) else feed_forward)(stage, nxt)

            run_network(pool, run)

        @block.scalar
        def _(act):
            def evacuate_q(a, n, par, c, bank=q_ps):
                act.wait_ge(q_in_psum, n + a.counts)
                nc.scalar.activation(qT[:, par, c, :], flat(bank)[:, 0:GN], ACT.Copy, scale=a.scale)\
                    .then_inc(q_ready, a.counts)

            def evacuate_v(a, n, par, v, bank):
                act.wait_ge(v_in_psum, n + a.counts)
                nc.scalar.activation(v_sb[0:a.keys, par, v // 2, (v % 2) * 512:(v % 2) * 512 + 512],
                                     bank[0:a.keys, :], ACT.Copy).then_inc(v_ready, a.counts)

            def exponentials(Q, q, keys):
                act.wait_ge(negmax_ready, Q + 1)
                if isinstance(Q, int) and Q < 2:
                    pass
                else:
                    act.wait_ge(pT_in_psum, Q - 1)
                for h in range(4):
                    e = nc.scalar.activation(probs[:, q % 2, h, 0:keys], score_ps[q % 2][:, h, 0:keys], ACT.Exp,
                                             bias=negmax[:, q % 2, h:h + 1], accum_out=sums[:, q % 2, h:h + 1])
                e.then_inc(exp_ready, 1)

            def evacuate_pT(Q, q, keys):
                act.wait_ge(pT_in_psum, Q + 1)
                nc.scalar.activation(pT[0:keys, q % 4, :, :], pT_ps[q % 2][0:keys, :, :], ACT.Copy)\
                    .then_inc(pT_ready, 1)

            def first_group(a):
                for c in range(a.chunks):
                    if c == 4:
                        exponentials(a.number * 64, 0, a.keys)
                    evacuate_q(a, a.number * 64 + c * a.counts, 0, c, (q_ps, pT_ps[0])[c % 2])
                if a.thin:
                    exponentials(a.number * 64, 0, a.keys)
                for v in range(0, 2 * GB, a.counts):
                    evacuate_v(a, a.number * 32 + v, 0, v, (y_ps, o_ps)[v // a.counts % 2])
                exponentials(a.number * 64 + 1, 1, a.keys)
                evacuate_pT(a.number * 64, 0, a.keys)

            def attention(a, nxt):
                def group(g, par, last):
                    Q = a.number * 64 + g * QUADS
                    b = nxt if last else a
                    on = isinstance(b, Attention)
                    for q in range(1, QUADS + 1):
                        for kind, i in items(ACT_THIN if a.thin else ACT_PLAN, q):
                            if kind == "e" and (q + 1 < QUADS or on):
                                exponentials(Q + (q + 1), q + 1, a.keys if q + 1 < QUADS else b.keys)
                            elif kind == "q" and on and i < b.chunks:
                                evacuate_q(b, a.number * 64 + (g + 1) * CH + i * b.counts, 1 - par, i)
                            elif kind == "v" and on and i % b.counts == 0:
                                evacuate_v(b, a.number * 32 + (g + 1) * 4 + i, 1 - par, i, y_ps)
                            elif kind == "p" and (q < QUADS or on):
                                evacuate_pT(Q + q, q, a.keys if q < QUADS else b.keys)

                with act.Fori(0, NG // 2 - 1) as p:
                    group(p * 2, 0, False)
                    group(p * 2 + 1, 1, False)
                group(NG - 2, 0, False)
                group(NG - 1, 1, True)

            def feed_forward(f, nxt):
                if f is FRONT[2]:
                    act.wait_ge(params_loaded, 48)
                nc.scalar.activation(hb[:, :], hbias[:, bass.ds(f.number, 1), :].rearrange("p a b -> p (a b)"),
                                     ACT.Copy).then_inc(hb_ready, 1)
                act.wait_ge(hb_ready, f.number + 1)

                def activate(g, par):
                    for c in range(FC):
                        n = f.number * 32 + g * FC + c
                        act.wait_ge(hidden_in_psum, n + 1)
                        if f.gated:
                            at_least(act, hid_ready, n - 1)
                            nc.scalar.activation(linear[:, c % 2, :], flat(pT_ps[c % 2])[:, 0:GN], ACT.Identity,
                                                 bias=hb[:, c:c + 1])
                        b = FC + c if f.gated else c
                        dst = gate[:, c % 2, :] if f.gated else hid[:, par, c, :]
                        bank = score_ps[c % 2] if f.gated else (*score_ps, *pT_ps)[c]
                        nc.scalar.activation(dst, flat(bank)[:, 0:GN], ACT.Gelu, bias=hb[:, b:b + 1])\
                            .then_inc(gate_ready if f.gated else hid_ready, 1)

                for g in range(NG):
                    activate(g, g % 2)
                if nxt is not None:
                    first_group(nxt)

            def run(stage, nxt):
                (attention if isinstance(stage, Attention) else feed_forward)(stage, nxt)

            first_group(FRONT[0])
            run_network(act, run)

        @block.vector
        def _(dve):
            def statistics(b, n, count, keep=None):
                for i in range(count):
                    src = x_rows[:, i, :] if keep is not None else xs[:, b + i, :]
                    op = nc.vector.bn_stats(bnst[:, i, :], src)
                op.then_inc(bn_ready, count)
                if keep is not None:
                    keep()
                hold(dve, bn_ready, n + count, dve_held)
                for i in range(count):
                    op = nc.vector.bn_aggr(mv_rows[:, i, :], bnst[:, i, :])
                op.then_inc(aggr_ready, count)
                hold(dve, aggr_ready, n + count, dve_held)
                return nc.vector.tensor_copy(mv[:, bass.ds(b, count), :], mv_rows[:, 0:count, :])

            def split_part(a, matrix, half):
                hold(dve, w_loaded, (a.number + 1) * (16 * QKV_DMAS), dve_held)
                n = a.number * W_PARTS + matrix * 2 + half
                cols = slice(half * 512, half * 512 + 512)

                def part(t):
                    return t.rearrange("p a n -> p (a n)")

                raw = part(w_raw[:, bass.ds(matrix, 1), cols])
                hi = part(w_hi[:, a.slot, bass.ds(matrix, 1), cols])
                lo = part(w_lo[:, a.slot, bass.ds(matrix, 1), cols])
                nc.vector.tensor_copy(hi, raw).then_inc(w_hi_ready, 1)
                dve.wait_ge(w_hi_ready, n + 1)
                nc.vector.tensor_tensor(lo, raw, hi, ALU.subtract).then_inc(w_split, 1)

            def split_w1(f):
                wide = (2 if f.gated else 1) * FF
                dve.wait_ge(ff_loaded, (f.number + 1) * (16 * FF_DMAS))
                nc.vector.tensor_copy(w1_hi[:, 0:wide], w1_raw[:, 0:wide]).then_inc(w1_hi_ready, 1)
                dve.wait_ge(w1_hi_ready, f.number + 1)
                nc.vector.tensor_tensor(w1_lo[:, 0:wide], w1_raw[:, 0:wide], w1_hi[:, 0:wide], ALU.subtract)\
                    .then_inc(w1_split, 1)

            def normalise_rows(st, g, pair):
                hold(dve, rstd_ready, st * (NG // 2) + pair + 1, dve_held)
                for i in range(GB):
                    b = g * GB + i
                    op = nc.vector.tensor_scalar(
                        xhat[:, i, :], xs[:, bass.ds(b, 1), :].rearrange("p a d -> p (a d)"),
                        mv[:, bass.ds(b, 1), 0:1].rearrange("p a d -> p (a d)"),
                        rstd[:, bass.ds(b, 1)], ALU.subtract, ALU.mult)
                op.then_inc(xhat_ready, 1)

            def take_hT(st, g, cross=False):
                N = st * NG + g
                dve.wait_ge(hT_in_psum, N + 1)
                gain = norm_sb[:, bass.ds(st, 1), 0:1].rearrange("p a d -> p (a d)")
                shift = norm_sb[:, bass.ds(st, 1), 1:2].rearrange("p a d -> p (a d)")
                nc.vector.tensor_scalar(hT[:, :], k_ps[:, 0:GN], gain, shift, ALU.mult, ALU.add)\
                    .then_inc(hT_affine, 1)
                if cross:
                    src = ctx_sb[:, bass.ds(g * (GB * T), GB * T)]
                    nc.vector.tensor_copy(c_hi[:, :], src)
                dve.wait_ge(hT_affine, N + 1)
                nc.vector.tensor_copy(h_hi[:, :], hT[:, :]).then_inc(h_hi_ready, 1)
                dve.wait_ge(h_hi_ready, N + 1)
                if cross:
                    nc.vector.tensor_tensor(c_lo[:, :], src, c_hi[:, :], ALU.subtract)
                nc.vector.tensor_tensor(h_lo[:, :], hT[:, :], h_hi[:, :], ALU.subtract).then_inc(hT_ready, 1)

            def update_x(st, b, count, stats_done, with_stats=True):
                n = st * B + b
                if not with_stats:
                    dve.wait_ge(x_updated, n)
                dve.wait_ge(y_in_psum, n + count)
                rows, new = xs[:, bass.ds(b, count), :], x_rows[:, 0:count, :]
                y = y_ps[:, 0:count * D].rearrange("p (b d) -> p b d", d=D)
                nc.vector.tensor_tensor(new, y, rows, ALU.add).then_inc(y_taken, count)

                def keep():
                    nc.vector.tensor_copy(rows, new).then_inc(x_updated, count)

                if not with_stats:
                    hold(dve, y_taken, n + count + 1, dve_held)
                    keep()
                    return
                dve.wait_ge(y_taken, n + count + 1)
                op = statistics(b, n + B, count, keep)
                if stats_done:
                    op.then_inc(stats_ready, 1)

            def row_max(Q, q, keys):
                dve.wait_ge(scores_ready, Q + 1)
                nc.vector.tensor_reduce(negmax[:, q % 2, :], score_ps[q % 2][:, :, 0:keys], AX.X, ALU.max,
                                        negate=True).then_inc(negmax_ready, 1)

            def inverse_sum(Q, q):
                dve.wait_ge(exp_ready, Q + 1)
                nc.vector.reciprocal(rinv[:, q % 2, :], sums[:, q % 2, :]).then_inc(rinv_ready, 1)

            def evacuate_k(a, n, par, c, bank=k_ps):
                dve.wait_ge(k_in_psum, n + a.counts)
                nc.vector.tensor_copy(kT[:, par, c, 0:GB * a.keys], flat(bank)[:, 0:GB * a.keys])\
                    .then_inc(k_ready, a.counts)

            def evacuate_out(a, n, m):
                dve.wait_ge(av_ready, n + 1)
                odd = m % 2
                rows, chunks = (slice(64 * odd, 64 * odd + 64), slice(0, 4)) if a.thin else \
                    (slice(0, 128), slice(4 * odd, 4 * odd + 4))
                nc.vector.tensor_copy(outT[rows, m // 2, chunks, :],
                                      o_ps[rows, :].rearrange("p (c s) -> p c s", c=4)).then_inc(outT_ready, 1)

            def ahead(st, g, last_pair, pair, nxt):
                if not last_pair:
                    return st, g + 2, pair + 1, g + 2
                if nxt is None:
                    return None
                return nxt.stage, g + 2 - NG, 0, g + 2 - NG

            def take_first_group(a, between=None):
                for c in range(a.chunks):
                    evacuate_k(a, a.number * 64 + c * a.counts, 0, c, (k_ps, pT_ps[1])[c % 2])
                    if c == 3:
                        row_max(a.number * 64, 0, a.keys)
                        row_max(a.number * 64 + 1, 1, a.keys)
                    if between is not None:
                        between(c)
                inverse_sum(a.number * 64, 0)
                take_hT(a.stage, 1, a.cross)
                row_max(a.number * 64 + 2, 2, a.keys)
                inverse_sum(a.number * 64 + 1, 1)

            def attention(a, nxt):
                following = next_attention(a, nxt)

                def group(g, par, pair, last_pair, last, part=None):
                    Q = a.number * 64 + g * QUADS
                    b = nxt if last else a
                    two_ahead = ahead(a.stage, g, last_pair, pair, nxt)
                    crossing = is_cross(nxt) if last_pair else a.cross
                    on = isinstance(b, Attention)
                    outputs = 0
                    for q in range(1, QUADS + 1):
                        for kind, c in items(DVE_THIN if a.thin else DVE_PLAN, q):
                            if kind == "m" and (q + 2 < QUADS or on):
                                row_max(Q + (q + 2), q + 2, a.keys if q + 2 < QUADS else b.keys)
                            elif kind == "x":
                                evacuate_out(a, a.number * 32 + g * 4 + (q // 2 - 1), q // 2 - 1)
                            elif kind == "k" and on and c < b.chunks:
                                evacuate_k(b, a.number * 64 + (g + 1) * CH + c * b.counts, 1 - par, c)
                            elif kind == "r" and (q + 1 < QUADS or on):
                                inverse_sum(Q + (q + 1), q + 1)
                            elif kind == "w":
                                if part is not None and following is not None:
                                    split_part(following, part, par)
                                if last_pair and not last and isinstance(nxt, FeedForward):
                                    split_w1(nxt)
                            elif kind == "n" and two_ahead is not None:
                                normalise_rows(two_ahead[0], two_ahead[1], two_ahead[2])
                            elif kind == "h":
                                if two_ahead is not None:
                                    take_hT(two_ahead[0], two_ahead[1], crossing)
                            elif kind == "u":
                                if outputs == 0:
                                    dve.wait_ge(xbias_ready, a.stage * NG + g + 1)
                                update_x(a.stage, g * GB + outputs, 1, outputs == 1)
                                outputs += 1

                with dve.Fori(0, NG // 2 - 1) as p:
                    group(p * 2, 0, p, False, False, p)
                    group(p * 2 + 1, 1, p, False, False, p)
                group(NG - 2, 0, NG // 2 - 1, True, False)
                group(NG - 1, 1, NG // 2 - 1, True, True)

            def feed_forward(f, nxt):
                def group(g, par, pair, last_pair, last):
                    if not last:
                        two_ahead = ahead(f.stage, g, last_pair, pair, nxt)
                        if two_ahead is not None:
                            take_hT(two_ahead[0], two_ahead[1], last_pair and nxt.cross)
                        if isinstance(g, int) and g + 3 >= NG:
                            if nxt is not None:
                                normalise_rows(nxt.stage, g + 3 - NG, 0)
                        else:
                            normalise_rows(f.stage, g + 3, pair + 1 + par)
                    elif nxt is not None:
                        take_first_group(nxt)
                    dve.wait_ge(xbias_ready, f.stage * NG + g + 1)
                    update_x(f.stage, g * GB, GB, True, nxt is not None)

                normalise_rows(f.stage, 2, 1)
                with dve.Fori(0, NG // 2 - 2) as p:
                    group(p * 2, 0, p, False, False)
                    group(p * 2 + 1, 1, p, False, False)
                for g in range(NG - 4, NG):
                    group(g, g % 2, g // 2, g >= NG - 2, g == NG - 1)

            dve.sem_inc(outT_ready, 1)
            dve.sem_inc(y_taken, 1)
            dve.wait_ge(first_loaded, 32)
            for b in range(0, 2 * GB, GB):
                statistics(b, b, GB).then_inc(stats_ready, 1)
            first = FRONT[0]
            for part in range(W_PARTS):
                split_part(first, part // 2, part % 2)
            normalise_rows(0, 0, 0)
            take_hT(0, 0)
            normalise_rows(0, 1, 0)

            def statistics_of_rest(c):
                if c == 0:
                    dve.wait_ge(x_loaded, 16)
                b = (2 + c) * GB
                if b < B:
                    statistics(b, b, GB).then_inc(stats_ready, 1)

            take_first_group(first, statistics_of_rest)
            dve.wait_ge(params_loaded, 48)

            def run(stage, nxt):
                (attention if isinstance(stage, Attention) else feed_forward)(stage, nxt)

            run_network(dve, run)

        @block.tensor
        def _(pe):
            pe.wait_ge(ident_ready, 1)

            def transpose_rows(st, g, k_before):
                N = st * NG + g
                pe.wait_ge(xhat_ready, N + 1)
                at_least(pe, k_ready, k_before)
                at_least(pe, hT_ready, N)
                for i in range(GB):
                    m = nc.tensor.transpose(k_ps[:, i * S:(i + 1) * S], xhat[:, i, :], ident[:, :])
                m.then_inc(hT_in_psum, 1)

            def three_passes(dst, l_hi, l_lo, r_hi, r_lo):
                nc.tensor.matmul(dst, l_hi, r_lo, start=True, stop=False)
                nc.tensor.matmul(dst, l_lo, r_hi, start=False, stop=False)
                return nc.tensor.matmul(dst, l_hi, r_hi, start=False, stop=True)

            def project_q(a, n, c, bank=q_ps, ahead=0):
                cols = slice(c * 128, c * 128 + 128)
                at_least(pe, q_ready, n - ahead)
                three_passes(flat(bank)[:, 0:GN], w_hi[:, a.slot, 0, cols], w_lo[:, a.slot, 0, cols], h_hi[:, :],
                             h_lo[:, :]).then_inc(q_in_psum, a.counts)

            def project_k(a, n, c, bank=k_ps, ahead=0):
                cols = slice(c * 128, c * 128 + 128)
                at_least(pe, k_ready, n - ahead)
                s_hi, s_lo = (c_hi, c_lo) if a.cross else (h_hi, h_lo)
                three_passes(flat(bank)[:, 0:GB * a.keys], w_hi[0:a.rows, a.slot, 1, cols], w_lo[0:a.rows, a.slot, 1, cols],
                             s_hi[:, :], s_lo[:, :]).then_inc(k_in_psum, a.counts)

            def project_v(a, n, v, y_before, bank=y_ps, ahead=0):
                s_hi, s_lo = (c_hi, c_lo) if a.cross else (h_hi, h_lo)
                i, cols = v // 2, slice((v % 2) * 512, (v % 2) * 512 + 512)
                rows = slice(i * a.keys, (i + 1) * a.keys)
                at_least(pe, v_ready, n - ahead)
                if not (isinstance(y_before, int) and y_before == 0):
                    pe.wait_ge(y_taken, y_before + 1)
                three_passes(bank[0:a.keys, :], s_hi[:, rows], s_lo[:, rows],
                             w_hi[0:a.rows, a.slot, 2, cols], w_lo[0:a.rows, a.slot, 2, cols])\
                    .then_inc(v_in_psum, a.counts)

            def scores(a, Q, q, par):
                if not isinstance(Q, int) or Q >= 2:
                    pe.wait_ge(exp_ready, Q - 1)
                i = (q // 4) % GB
                for h in range(4):
                    c, lo = a.head_of(q, h)
                    m = nc.tensor.matmul(score_ps[q % 2][:, h, 0:a.keys],
                                         qT[lo:lo + a.space, par, c, i * S:(i + 1) * S],
                                         kT[lo:lo + a.space, par, c, i * a.keys:(i + 1) * a.keys],
                                         start=True, stop=True)
                m.then_inc(scores_ready, 1)

            def transpose_probs(Q, q, keys):
                pe.wait_ge(probs_ready, Q + 1)
                for h in range(4):
                    m = nc.tensor.transpose(pT_ps[q % 2][0:keys, h, :], probs[:, q % 2, h, 0:keys], ident[:, :])
                m.then_inc(pT_in_psum, 1)

            def weigh_values(a, Q, n, q, par):
                pe.wait_ge(pT_ready, Q + 2)
                pe.wait_ge(outT_ready, n + 1)
                for h in range(4):
                    for odd in range(2):
                        c, lo = a.head_of(q + odd, h)
                        m = nc.tensor.matmul(o_ps[lo:lo + a.space, h * S:(h + 1) * S],
                                             v_sb[0:a.keys, par, q // 4, c * 128 + lo:c * 128 + lo + a.space],
                                             pT[0:a.keys, (q + odd) % 4, h, :], start=True, stop=True)
                m.then_inc(av_ready, 1)

            def project_out(a, b, pairs_done, slot, v_before):
                thin_before = 0 if isinstance(a.turn, int) and a.turn == 0 else 16 * WO_DMAS
                pe.wait_ge(wo_loaded[a.slot], (a.turn + 1) * (16 * WO_DMAS) + thin_before)
                pe.wait_ge(outT_ready, pairs_done + 1)
                pe.wait_ge(y_taken, a.stage * B + b + 1)
                at_least(pe, v_ready, v_before)
                for c in range(a.chunks):
                    m = nc.tensor.matmul(y_ps[:, 0:D], outT[:, slot, c, :], wo_sb[:, a.slot, c, :],
                                         start=(c == 0), stop=(c == a.chunks - 1))
                m.then_inc(y_in_psum, 1)

            def start_attention(a):
                pe.wait_ge(hT_ready, a.stage * NG + 1)
                pe.wait_ge(w_split, (a.number + 1) * W_PARTS)
                for c in range(a.chunks):
                    n = a.number * 64 + c * a.counts
                    project_q(a, n, c, (q_ps, pT_ps[0])[c % 2], a.counts)
                    project_k(a, n, c, (k_ps, pT_ps[1])[c % 2], a.counts)
                    if c == 3:
                        pe.wait_ge(q_ready, a.number * 64 + 4 * a.counts)
                        pe.wait_ge(k_ready, a.number * 64 + 4 * a.counts)
                        for q in range(2):
                            scores(a, a.number * 64 + q, q, 0)
                if not a.thin:
                    pe.wait_ge(q_ready, a.number * 64 + CH)
                    pe.wait_ge(k_ready, a.number * 64 + CH)
                for v in range(0, 2 * GB, a.counts):
                    project_v(a, a.number * 32 + v, v, 0, (y_ps, o_ps)[v // a.counts % 2], a.counts)
                transpose_rows(a.stage, 1, a.number * 64 + CH)
                scores(a, a.number * 64 + 2, 2, 0)
                transpose_probs(a.number * 64, 0, a.keys)

            def attention(a, nxt):
                k0, v0 = a.number * 64, a.number * 32
                def group(g, par, last_pair, last):
                    Q = a.number * 64 + g * QUADS
                    n = a.number * 32 + g * 4
                    b = nxt if last else a
                    on = isinstance(b, Attention)
                    v_after = v0 + (g + 1) * 4
                    outputs = pieces = 0
                    for q in range(1, QUADS + 1):
                        if q == 1:
                            pe.wait_ge(v_ready, v0 + g * 4 + 4)
                            if on:
                                pe.wait_ge(hT_ready, a.stage * NG + g + 2)
                                if last:
                                    pe.wait_ge(w_split, (nxt.number + 1) * W_PARTS)
                        for kind, i in items(PE_THIN if a.thin else PE_PLAN, q):
                            if kind == "s":
                                if q in (QUADS - 2, QUADS) and on:
                                    needed = k0 + (g + 1) * CH + (4 * b.counts if q < QUADS else CH)
                                    pe.wait_ge(q_ready, needed)
                                    pe.wait_ge(k_ready, needed)
                                if q + 2 < QUADS:
                                    scores(a, Q + (q + 2), q + 2, par)
                                elif on:
                                    scores(b, Q + (q + 2), q + 2, 1 - par)
                            elif kind == "a":
                                weigh_values(a, Q + (q - 2), n + (q // 2 - 1), q - 2, par)
                            elif kind == "q" and on and i < b.chunks:
                                project_q(b, k0 + (g + 1) * CH + i * b.counts, i)
                            elif kind == "k" and on and i < b.chunks:
                                project_k(b, k0 + (g + 1) * CH + i * b.counts, i)
                            elif kind == "v" and on and i % b.counts == 0:
                                project_v(b, v_after + i, i, a.stage * B + g * GB + outputs)
                                pieces += b.counts
                            elif kind == "h":
                                if isinstance(b, FeedForward):
                                    start_hidden(b)
                                if not last_pair:
                                    transpose_rows(a.stage, g + 2, k0 + (g + 2) * CH)
                                elif nxt is not None:
                                    transpose_rows(nxt.stage, g + 2 - NG, k0 + (g + 1) * CH + (CH if on else 0))
                            elif kind == "t" and (q < QUADS or on):
                                transpose_probs(Q + q, q, a.keys if q < QUADS else b.keys)
                            elif kind == "o":
                                project_out(a, g * GB + outputs, n + 2 * (outputs + 1), outputs, v_after + pieces)
                                outputs += 1

                with pe.Fori(0, NG // 2 - 1) as p:
                    group(p * 2, 0, False, False)
                    group(p * 2 + 1, 1, False, False)
                group(NG - 2, 0, True, False)
                group(NG - 1, 1, True, True)

            def hidden(f, g):
                pe.wait_ge(hT_ready, f.stage * NG + g + 1)
                for c in range(FC):
                    n = f.number * 32 + g * FC + c
                    if f.gated:
                        at_least(pe, gate_ready, gates_before(f) + g * FC + c - 1)
                    elif not isinstance(n, int) or n > 3:
                        pe.wait_ge(hid_ready, n - 3)
                    if f.gated:
                        cols = slice(c * 128, c * 128 + 128)
                        three_passes(flat(pT_ps[c % 2])[:, 0:GN], w1_hi[:, cols], w1_lo[:, cols], h_hi[:, :], h_lo[:, :])
                    b = FC + c if f.gated else c
                    cols = slice(b * 128, b * 128 + 128)
                    bank = score_ps[c % 2] if f.gated else (*score_ps, *pT_ps)[c]
                    three_passes(flat(bank)[:, 0:GN], w1_hi[:, cols], w1_lo[:, cols], h_hi[:, :], h_lo[:, :])\
                        .then_inc(hidden_in_psum, 1)

            def start_hidden(f):
                pe.wait_ge(w1_split, f.number + 1)
                pe.wait_ge(exp_ready, f.attentions * 64)
                pe.wait_ge(pT_ready, f.attentions * 64)
                hidden(f, 0)

            def feed_forward(f, nxt):
                k0, v0 = f.attentions * 64, f.attentions * 32

                def second(g, par):
                    pe.wait_ge(ff_loaded, (f.number + 1) * (16 * FF_DMAS))
                    pe.wait_ge(hid_ready, f.number * 32 + g * FC + FC)
                    pe.wait_ge(y_taken, f.stage * B + g * GB + 1)
                    for i in range(GB):
                        for c in range(FC):
                            m = nc.tensor.matmul(y_ps[:, i * D:(i + 1) * D], hid[:, par, c, i * S:(i + 1) * S],
                                                 w2_sb[:, c, :], start=(c == 0), stop=(c == FC - 1))
                    m.then_inc(y_in_psum, GB)

                def group(g, par, last_pair, last):
                    if not last:
                        hidden(f, g + 1)
                        if not last_pair:
                            transpose_rows(f.stage, g + 2, k0)
                        elif nxt is not None:
                            transpose_rows(nxt.stage, g + 2 - NG, k0)
                    elif nxt is not None:
                        pe.wait_ge(y_taken, f.stage * B + g * GB + 1)
                        pe.wait_ge(hid_ready, f.number * 32 + g * FC + FC)
                        start_attention(nxt)
                        pe.wait_ge(v_ready, v0 + 4)
                    second(g, par)

                with pe.Fori(0, NG // 2 - 1) as p:
                    group(p * 2, 0, False, False)
                    group(p * 2 + 1, 1, False, False)
                group(NG - 2, 0, True, False)
                group(NG - 1, 1, True, True)

            transpose_rows(0, 0, 0)
            start_attention(FRONT[0])

            def run(stage, nxt):
                (attention if isinstance(stage, Attention) else feed_forward)(stage, nxt)

            run_network(pe, run)


def kernel(**inputs):
    import numpy as np
    from concourse.bacc import Bacc
    from concourse.bass_utils import run_bass_kernel_spmd

    nc = Bacc("TRN2", target_bir_lowering=False, num_devices=1)
    arrays = {}

    def dram(name, a):
        a = np.ascontiguousarray(a)
        arrays[name] = a
        return nc.dram_tensor(name, a.shape, mybir.dt.from_np(a.dtype), kind="ExternalInput").ap()

    def given(name):
        return dram(name, inputs[name])

    L0, L1, L2, L3 = (f"L{i}_xattn_" for i in range(4))
    pairs = [(L0 + "ln1_g", L0 + "ln1_b"), (L0 + "ln2_g", L0 + "ln2_b"), (L0 + "ln3_g", L0 + "ln3_b"),
             (L1 + "n1_g", L1 + "n1_b"), (L1 + "n2_g", L1 + "n2_b"), (L1 + "n3_g", L1 + "n3_b"),
             (L1 + "n4_g", L1 + "n4_b"),
             (L2 + "g1", L2 + "be1"), (L2 + "g2", L2 + "be2"), (L2 + "g3", L2 + "be3")]
    biases = [L0 + "sa_bo", L0 + "ca_bo", L0 + "ff_b2", L1 + "so_b", L1 + "f1_b2", L1 + "co_b", L1 + "f2_b2",
              L2 + "bo1", L2 + "bo2", L2 + "b2"]
    gains = [np.asarray(inputs[g]) for g, _ in pairs]
    shifts = [np.asarray(inputs[b]) for _, b in pairs]
    rows = [np.asarray(inputs[b]) for b in biases]
    for i in range(DEPTH3):
        for n, b in (("ln1", "b_sa_o"), ("ln2", "b_ca_o"), ("ln3", "b_ff2")):
            gains.append(np.asarray(inputs[f"{L3}{n}_g"])[i])
            shifts.append(np.asarray(inputs[f"{L3}{n}_b"])[i])
            rows.append(np.asarray(inputs[L3 + b])[i])
    norms = dram("norms", np.stack([np.stack(gains, 1), np.stack(shifts, 1)], 2))
    out_biases = dram("out_biases", np.stack(rows))
    hidden = []
    for b in (inputs[L0 + "ff_b1"], inputs[L1 + "f1_b1"], inputs[L1 + "f2_b1"], inputs[L2 + "bp"],
              *np.asarray(inputs[L3 + "b_ff1"])):
        h = np.zeros((128, 2 * FC), np.float32)
        h[:, :len(b) // 128] = np.asarray(b).reshape(-1, 128).T
        hidden.append(h)
    hidden_biases = dram("hidden_biases", np.stack(hidden, 1))
    ctxT = dram("ctxT", np.asarray(inputs["ctx_768"]).transpose(2, 0, 1).reshape(C, B * T))

    attn_w = {
        0: [given(L0 + n) for n in ("sa_wq", "sa_wk", "sa_wv", "sa_wo")],
        1: [given(L0 + n) for n in ("ca_wq", "ca_wk", "ca_wv", "ca_wo")],
        4: [given(L2 + n) for n in ("Wq1", "Wk1", "Wv1", "Wo1")],
        5: [given(L2 + n) for n in ("Wq2", "Wk2", "Wv2", "Wo2")],
    }
    thin_w = {"self": [given(L1 + n) for n in ("sq_w", "sk_w", "sv_w", "so_w")],
              "cross": [given(L1 + n) for n in ("cq_w", "ck_w", "cv_w", "co_w")]}
    ff_w = {0: (given(L0 + "ff_w1"), given(L0 + "ff_w2")), 1: (given(L1 + "f1_w1"), given(L1 + "f1_w2")),
            2: (given(L1 + "f2_w1"), given(L1 + "f2_w2")), 3: (given(L2 + "Wp"), given(L2 + "W2"))}
    qkv, sao, wq, kv, cao, ff1, ff2 = (given(L3 + n) for n in
                                       ("w_qkv", "w_sa_o", "w_q", "w_kv", "w_ca_o", "w_ff1", "w_ff2"))

    def of_layer(w, lo=None, hi=None):
        cols = slice(0, w.shape[2]) if lo is None else slice(lo, hi)
        return lambda layer: w[bass.ds(layer, 1), :, cols].rearrange("a p n -> (a p) n")

    deep_w = {
        "self": [of_layer(qkv, 0, INNER), of_layer(qkv, INNER, 2 * INNER), of_layer(qkv, 2 * INNER, 3 * INNER),
                 of_layer(sao)],
        "cross": [of_layer(wq), of_layer(kv, 0, INNER), of_layer(kv, INNER, 2 * INNER), of_layer(cao)],
        "ff": [of_layer(ff1), of_layer(ff2)],
    }
    out = nc.dram_tensor("out", (B, S, D), F32, kind="ExternalOutput").ap()
    build(nc, given("x"), ctxT, norms, out_biases, hidden_biases, attn_w, thin_w, ff_w, deep_w, out)
    r = run_bass_kernel_spmd(nc, [arrays], core_ids=[0])
    return r.results[0]["out"]
```
